# Optimizing a Trainium2 kernel written in Bass

```python
import numpy as np
import jax
import jax.numpy as jnp

def _softmax(x, axis=-1):
    return jax.nn.softmax(x, axis=axis)

def _gelu(x):
    return jax.nn.gelu(x, approximate=True)

def _silu(x):
    return jax.nn.silu(x)

def _sigmoid(x):
    return jax.nn.sigmoid(x)

def _layernorm(x, axis=-1, eps=1e-05):
    m = jnp.mean(x, axis=axis, keepdims=True)
    v = jnp.var(x, axis=axis, keepdims=True)
    return (x - m) / jnp.sqrt(v + eps)

def _scatter_add(tgt, idx, src, axis=0):
    return tgt.at[idx].add(src)

def _segment_sum(src, seg, n):
    return jax.ops.segment_sum(src, seg, n)
kernel_name = 'mk_cond_seq_d2_seqx_r8_6b625c'

def setup_inputs(seed: int=0):
    np.random.seed(seed)
    _w = jnp.asarray

    def _rec_inputs():
        import jax
        import jax.numpy as jnp
        _rk = jax.random.key(seed)
        x = -0.0003482 + 1 * jax.random.normal(jax.random.fold_in(_rk, 1), (16, 128, 144), jnp.float32)
        _lenS = 128 - jax.random.randint(jax.random.fold_in(_rk, 7), (16,), 0, max(1, 128 // 4) + 1, jnp.int32)
        _lenS2 = 128 - jax.random.randint(jax.random.fold_in(_rk, 8), (16,), 0, max(1, 128 // 4) + 1, jnp.int32)
        cond_1152 = -0.00342701 + 1.00097 * jax.random.normal(jax.random.fold_in(_rk, 11), (16, 144), jnp.float32)
        return (x, cond_1152)
    x, cond_1152 = _rec_inputs()

    def _L0_cond_setup():
        import jax, jax.numpy as jnp
        import numpy as np
        B, T, D, H = (64, 32, 144, 16)
        HD = D // H
        EPS = 1e-06

        def _ln(x):
            mu = jnp.mean(x, axis=-1, keepdims=True)
            var = jnp.var(x, axis=-1, keepdims=True)
            return (x - mu) * jax.lax.rsqrt(var + EPS)

        def _modulate(x, shift, scale):
            return x * (1.0 + scale[:, None, :]) + shift[:, None, :]

        def _attn(x, Wq, Wk, Wv, Wp, bp):
            b, t, d = x.shape
            q = (x @ Wq).reshape(b, t, H, HD).transpose(0, 2, 1, 3)
            k = (x @ Wk).reshape(b, t, H, HD).transpose(0, 2, 1, 3)
            v = (x @ Wv).reshape(b, t, H, HD).transpose(0, 2, 1, 3)
            scores = jnp.einsum('bhqd,bhkd->bhqk', q, k) / np.sqrt(HD)
            mask = jnp.triu(jnp.ones((t, t), bool), k=1)
            scores = jnp.where(mask, -jnp.inf, scores)
            w = jax.nn.softmax(scores, axis=-1)
            ctx = jnp.einsum('bhqk,bhkd->bhqd', w, v).transpose(0, 2, 1, 3).reshape(b, t, d)
            return ctx @ Wp + bp

        def _mlp(x, W1, b1, W2, b2):
            return jax.nn.silu(x @ W1 + b1) @ W2 + b2
        key = jax.random.key(seed)
        ks = jax.random.split(key, 12)
        s = lambda fan_in: 1.0 / np.sqrt(fan_in)
        return {'x': jax.random.normal(ks[0], (B, T, D), jnp.float32), 'c': jax.random.normal(ks[1], (B, D), jnp.float32), 'Wq': jax.random.normal(ks[2], (D, D), jnp.float32) * s(D), 'Wk': jax.random.normal(ks[3], (D, D), jnp.float32) * s(D), 'Wv': jax.random.normal(ks[4], (D, D), jnp.float32) * s(D), 'Wp': jax.random.normal(ks[5], (D, D), jnp.float32) * s(D), 'bp': jnp.zeros((D,), jnp.float32), 'W1': jax.random.normal(ks[6], (D, 4 * D), jnp.float32) * s(D), 'b1': jnp.zeros((4 * D,), jnp.float32), 'W2': jax.random.normal(ks[7], (4 * D, D), jnp.float32) * s(4 * D), 'b2': jnp.zeros((D,), jnp.float32), 'Wa': jax.random.normal(ks[8], (D, 6 * D), jnp.float32) * s(D), 'ba': jnp.zeros((6 * D,), jnp.float32)}
    _L0_cond_all = _L0_cond_setup()
    _L0_cond_in = {k: v for k, v in _L0_cond_all.items() if k in ('Wq', 'Wk', 'Wv', 'Wp', 'bp', 'W1', 'b1', 'W2', 'b2', 'Wa', 'ba')}
    del _L0_cond_all

    def _L1_cond_setup():
        import jax, jax.numpy as jnp
        import numpy as np
        B, L, C = (8, 128, 144)
        H = 16
        D = C // H
        FF = int(C * 4.0)
        EPS = 1e-06

        def _layernorm(x):
            mu = jnp.mean(x, axis=-1, keepdims=True)
            var = jnp.mean(jnp.square(x - mu), axis=-1, keepdims=True)
            return (x - mu) * jax.lax.rsqrt(var + EPS)

        def _modulate(x, shift, scale):
            return x * (1.0 + scale) + shift

        def _attention(h, W_qkv, b_qkv, W_proj, b_proj):
            b, l, c = h.shape
            qkv = h @ W_qkv + b_qkv
            qkv = qkv.reshape(b, l, 3, H, D)
            q, k, v = (qkv[:, :, 0], qkv[:, :, 1], qkv[:, :, 2])
            scale = D ** (-0.5)
            scores = jnp.einsum('blhd,bmhd->bhlm', q * scale, k)
            attn = jax.nn.softmax(scores, axis=-1)
            o = jnp.einsum('bhlm,bmhd->blhd', attn, v).reshape(b, l, c)
            return o @ W_proj + b_proj
        key = jax.random.key(seed)
        ks = jax.random.split(key, 12)
        s = 0.02
        return {'x': jax.random.normal(ks[0], (B, L, C), jnp.float32), 'c': jax.random.normal(ks[1], (B, 1, C), jnp.float32), 'W_qkv': jax.random.normal(ks[2], (C, 3 * C), jnp.float32) * s, 'b_qkv': jnp.zeros((3 * C,), jnp.float32), 'W_proj': jax.random.normal(ks[3], (C, C), jnp.float32) * s, 'b_proj': jnp.zeros((C,), jnp.float32), 'W_fc1': jax.random.normal(ks[4], (C, FF), jnp.float32) * s, 'b_fc1': jnp.zeros((FF,), jnp.float32), 'W_fc2': jax.random.normal(ks[5], (FF, C), jnp.float32) * s, 'b_fc2': jnp.zeros((C,), jnp.float32), 'W_ada': jax.random.normal(ks[6], (C, 6 * C), jnp.float32) * s, 'b_ada': jnp.zeros((6 * C,), jnp.float32)}
    _L1_cond_all = _L1_cond_setup()
    _L1_cond_in = {k: v for k, v in _L1_cond_all.items() if k in ('W_qkv', 'b_qkv', 'W_proj', 'b_proj', 'W_fc1', 'b_fc1', 'W_fc2', 'b_fc2', 'W_ada', 'b_ada')}
    del _L1_cond_all
    return {'x': x, 'cond_1152': cond_1152, 'L0_cond_Wq': _L0_cond_in['Wq'], 'L0_cond_Wk': _L0_cond_in['Wk'], 'L0_cond_Wv': _L0_cond_in['Wv'], 'L0_cond_Wp': _L0_cond_in['Wp'], 'L0_cond_bp': _L0_cond_in['bp'], 'L0_cond_W1': _L0_cond_in['W1'], 'L0_cond_b1': _L0_cond_in['b1'], 'L0_cond_W2': _L0_cond_in['W2'], 'L0_cond_b2': _L0_cond_in['b2'], 'L0_cond_Wa': _L0_cond_in['Wa'], 'L0_cond_ba': _L0_cond_in['ba'], 'L1_cond_W_qkv': _L1_cond_in['W_qkv'], 'L1_cond_b_qkv': _L1_cond_in['b_qkv'], 'L1_cond_W_proj': _L1_cond_in['W_proj'], 'L1_cond_b_proj': _L1_cond_in['b_proj'], 'L1_cond_W_fc1': _L1_cond_in['W_fc1'], 'L1_cond_b_fc1': _L1_cond_in['b_fc1'], 'L1_cond_W_fc2': _L1_cond_in['W_fc2'], 'L1_cond_b_fc2': _L1_cond_in['b_fc2'], 'L1_cond_W_ada': _L1_cond_in['W_ada'], 'L1_cond_b_ada': _L1_cond_in['b_ada']}

def reference(x, cond_1152, L0_cond_Wq, L0_cond_Wk, L0_cond_Wv, L0_cond_Wp, L0_cond_bp, L0_cond_W1, L0_cond_b1, L0_cond_W2, L0_cond_b2, L0_cond_Wa, L0_cond_ba, L1_cond_W_qkv, L1_cond_b_qkv, L1_cond_W_proj, L1_cond_b_proj, L1_cond_W_fc1, L1_cond_b_fc1, L1_cond_W_fc2, L1_cond_b_fc2, L1_cond_W_ada, L1_cond_b_ada):
    import jax
    import jax.numpy as jnp

    def _L0_cond_ref(x, c, Wq, Wk, Wv, Wp, bp, W1, b1, W2, b2, Wa, ba):
        import jax, jax.numpy as jnp
        import numpy as np
        B, T, D, H = (64, 32, 144, 16)
        HD = D // H
        EPS = 1e-06

        def _ln(x):
            mu = jnp.mean(x, axis=-1, keepdims=True)
            var = jnp.var(x, axis=-1, keepdims=True)
            return (x - mu) * jax.lax.rsqrt(var + EPS)

        def _modulate(x, shift, scale):
            return x * (1.0 + scale[:, None, :]) + shift[:, None, :]

        def _attn(x, Wq, Wk, Wv, Wp, bp):
            b, t, d = x.shape
            q = (x @ Wq).reshape(b, t, H, HD).transpose(0, 2, 1, 3)
            k = (x @ Wk).reshape(b, t, H, HD).transpose(0, 2, 1, 3)
            v = (x @ Wv).reshape(b, t, H, HD).transpose(0, 2, 1, 3)
            scores = jnp.einsum('bhqd,bhkd->bhqk', q, k) / np.sqrt(HD)
            mask = jnp.triu(jnp.ones((t, t), bool), k=1)
            scores = jnp.where(mask, -jnp.inf, scores)
            w = jax.nn.softmax(scores, axis=-1)
            ctx = jnp.einsum('bhqk,bhkd->bhqd', w, v).transpose(0, 2, 1, 3).reshape(b, t, d)
            return ctx @ Wp + bp

        def _mlp(x, W1, b1, W2, b2):
            return jax.nn.silu(x @ W1 + b1) @ W2 + b2
        mod = jax.nn.silu(c) @ Wa + ba
        sh_msa, sc_msa, g_msa, sh_mlp, sc_mlp, g_mlp = jnp.split(mod, 6, axis=1)
        x = x + g_msa[:, None, :] * _attn(_modulate(_ln(x), sh_msa, sc_msa), Wq, Wk, Wv, Wp, bp)
        x = x + g_mlp[:, None, :] * _mlp(_modulate(_ln(x), sh_mlp, sc_mlp), W1, b1, W2, b2)
        return x

    def _L1_cond_ref(x, c, W_qkv, b_qkv, W_proj, b_proj, W_fc1, b_fc1, W_fc2, b_fc2, W_ada, b_ada):
        import jax, jax.numpy as jnp
        import numpy as np
        B, L, C = (8, 128, 144)
        H = 16
        D = C // H
        FF = int(C * 4.0)
        EPS = 1e-06

        def _layernorm(x):
            mu = jnp.mean(x, axis=-1, keepdims=True)
            var = jnp.mean(jnp.square(x - mu), axis=-1, keepdims=True)
            return (x - mu) * jax.lax.rsqrt(var + EPS)

        def _modulate(x, shift, scale):
            return x * (1.0 + scale) + shift

        def _attention(h, W_qkv, b_qkv, W_proj, b_proj):
            b, l, c = h.shape
            qkv = h @ W_qkv + b_qkv
            qkv = qkv.reshape(b, l, 3, H, D)
            q, k, v = (qkv[:, :, 0], qkv[:, :, 1], qkv[:, :, 2])
            scale = D ** (-0.5)
            scores = jnp.einsum('blhd,bmhd->bhlm', q * scale, k)
            attn = jax.nn.softmax(scores, axis=-1)
            o = jnp.einsum('bhlm,bmhd->blhd', attn, v).reshape(b, l, c)
            return o @ W_proj + b_proj
        ada = jax.nn.silu(c) @ W_ada + b_ada
        shift_msa, scale_msa, gate_msa, shift_mlp, scale_mlp, gate_mlp = jnp.split(ada, 6, axis=-1)
        h = _modulate(_layernorm(x), shift_msa, scale_msa)
        x = x + gate_msa * _attention(h, W_qkv, b_qkv, W_proj, b_proj)
        h = _modulate(_layernorm(x), shift_mlp, scale_mlp)
        mlp = jax.nn.gelu(h @ W_fc1 + b_fc1, approximate=True) @ W_fc2 + b_fc2
        x = x + gate_mlp * mlp
        return x
    x = _L0_cond_ref(x, cond_1152, L0_cond_Wq, L0_cond_Wk, L0_cond_Wv, L0_cond_Wp, L0_cond_bp, L0_cond_W1, L0_cond_b1, L0_cond_W2, L0_cond_b2, L0_cond_Wa, L0_cond_ba)
    x = _L1_cond_ref(x, cond_1152[:, None, :], L1_cond_W_qkv, L1_cond_b_qkv, L1_cond_W_proj, L1_cond_b_proj, L1_cond_W_fc1, L1_cond_b_fc1, L1_cond_W_fc2, L1_cond_b_fc2, L1_cond_W_ada, L1_cond_b_ada)
    return x

_drawn_inputs = setup_inputs


def setup_inputs(seed=0):
    import zlib

    import numpy as np

    out = dict(_drawn_inputs(seed))
    spreads = {'L0_cond_bp': (0.0, 0.1),
     'L0_cond_b1': (0.0, 0.1),
     'L0_cond_b2': (0.0, 0.1),
     'L0_cond_ba': (0.0, 0.1),
     'L1_cond_b_qkv': (0.0, 0.8),
     'L1_cond_b_proj': (0.0, 0.607),
     'L1_cond_b_fc1': (0.0, 0.8),
     'L1_cond_b_fc2': (0.0, 0.561),
     'L1_cond_b_ada': (0.0, 0.64)}
    factors = {'L1_cond_W_qkv': 8.0,
     'L1_cond_W_proj': 8.0,
     'L1_cond_W_fc1': 6.537,
     'L1_cond_W_fc2': 5.988,
     'L1_cond_W_ada': 3.263}
    for name, (base, spread) in spreads.items():
        noise = np.random.default_rng([zlib.crc32(name.encode()), seed]).standard_normal(out[name].shape)
        drawn = base * np.exp(spread * noise) if base else spread * noise
        out[name] = jnp.asarray(drawn.astype(out[name].dtype))
    for name, factor in factors.items():
        out[name] = (out[name] * factor).astype(out[name].dtype)
    return out
```

```python
from contextlib import ExitStack

import concourse.bass as bass
from concourse import mybir

F32 = mybir.dt.float32
F16 = mybir.dt.float16
BF16 = mybir.dt.bfloat16
ALU = mybir.AluOpType
ACT = mybir.ActivationFunctionType
AX_X = mybir.AxisListType.X

B, T, D = 16, 128, 144
H = 16
HD = D // H
FF = 4 * D
EPS = 1e-6
PAIRS = B // 2
TOK = 2 * T

NJ, NG = 4, 4
SLOT = 128 // NJ
PARTS = 3 * HD
MROW = PARTS
MS = 64.0

CH = 4
KR = 109
CAT = CH * KR
QK, VC = 2 * NG * 128, D
WCOLS = QK + VC + FF
WS = 16.0
HALF = D // 2
FCH = (FF + 127) // 128
FLAST = FF - 128 * (FCH - 1)
MOD = 6 * D
MREP = 96


def at(pair, per_pair, k):
    return pair * per_pair + k


def wait(eng, sem, value):
    if not (isinstance(value, int) and value <= 0):
        eng.wait_ge(sem, value)


def two_layer_kernel(nc, x, c_rep, w_cat, w_proj, w_fc2, w_ada, wmask, qkmask, batch_sel, out):
    ctx = ExitStack()
    with ctx:
        def sb(name, shape, dt):
            return ctx.enter_context(nc.sbuf_tensor(name, shape, dt))

        def sem(name):
            return ctx.enter_context(nc.semaphore(name))

        def per_layer(make, name):
            return [make(f"{name}{l}") for l in range(2)]

        ident = sb("ident", [128, 128], F32)
        ident16 = sb("ident16", [128, 128], F16)
        identb = sb("identb", [128, 128], BF16)
        causal = sb("causal", [128, NG, 128], BF16)
        sel = sb("sel", [MREP, B, 128], BF16)
        selc = sb("selc", [MREP, B], F32)
        wmask_sb = sb("wmask_sb", [KR, CH], F32)
        qkmask_sb = sb("qkmask_sb", [128, 2], F32)
        c_sb = sb("c_sb", [HALF + 1, 2, MREP], F32)
        sc_sb = sb("sc_sb", [HALF + 1, 2, MREP], F32)
        w_raw = [sb(f"w_raw{l}", [KR, CH, WCOLS], F32) for l in range(2)]
        w_t = sb("w_t", [KR, WCOLS], F16)
        w16 = [sb(f"w16_{l}", [KR, CH, WCOLS], F16) for l in range(2)]
        wp_sb = [sb(f"wp_sb{l}", [HALF + 1, 2, D], F32) for l in range(2)]
        w2_sb = [sb(f"w2_sb{l}", [128, FCH, D], F32) for l in range(2)]
        wa_sb = [sb(f"wa_sb{l}", [HALF + 1, 2, MOD], F32) for l in range(2)]
        mod_f = [sb(f"mod_f{l}", [MREP, MOD], F32) for l in range(2)]
        mod_r = sb("mod_r", [MREP, MOD], F32)
        mod_b = [sb(f"mod_b{l}", [MREP, MOD], BF16) for l in range(2)]

        x_in = [sb(f"x_in{l}", [128, 2, D], F32) for l in range(2)]
        x_mid = [sb(f"x_mid{l}", [128, 2, D], F32) for l in range(2)]
        x_fin = sb("x_fin", [128, 2, D], F32)
        gated = [sb(f"gated{l}", [128, 2, D], F32) for l in range(2)]
        stats = [sb(f"stats{l}", [128, 2, 6], F32) for l in range(2)]
        mv = [sb(f"mv{l}", [128, 2, 2], F32) for l in range(2)]
        veps = [sb(f"veps{l}", [128, 2], F32) for l in range(2)]
        minus_half = sb("minus_half", [128, 2], F32)
        eps_sb = sb("eps_sb", [128, 2], F32)
        rstd = [sb(f"rstd{l}", [128, 2], F32) for l in range(2)]
        ln_t = [sb(f"ln_t{l}", [128, 2, D], F32) for l in range(2)]
        ln_h = [sb(f"ln_h{l}", [128, 2, D], F32) for l in range(2)]
        h_cat = [sb(f"h_cat{l}", [128, 2, CAT], F16) for l in range(2)]
        hT = [sb(f"hT{l}", [KR, CH, TOK], F16) for l in range(2)]
        v_aug = [sb(f"v_aug{l}", [128, 2, H, HD + 1], F32) for l in range(2)]
        qk_lo = [sb(f"qk_lo{l}", [128, 4, 2 * TOK], F16) for l in range(2)]
        qkT = [sb(f"qkT{l}", [128, 2 * NG, TOK], F16) for l in range(2)]
        mx = [sb(f"mx{l}", [128, 2, NJ, NG], F32) for l in range(2)]
        mneg = [sb(f"mneg{l}", [128, 2, NG, NJ], F16) for l in range(2)]
        mrow = [[sb(f"mrow{l}{b}", [NJ, NG, 128], F16) for b in range(2)] for l in range(2)]
        probs = [[sb(f"probs{l}{k}", [128, 2, NG, 128], F32) for k in range(2)] for l in range(2)]
        oT = [sb(f"oT{l}", [128, NG, 128], F32) for l in range(2)]
        rden = [sb(f"rden{l}", [128, 2, H], F32) for l in range(2)]
        o_nat = [sb(f"o_nat{l}", [128, 2, 2, HALF + 1], F32) for l in range(2)]
        onT = [sb(f"onT{l}", [HALF + 1, 2, 2, 128], F32) for l in range(2)]
        ffT = [sb(f"ffT{l}", [128, FCH, TOK], F32) for l in range(2)]
        ps = [ctx.enter_context(nc.psum_tensor(f"ps{l}", [128, 4, 512], F32)) for l in range(2)]

        const_in, sel_in, c_in = sem("const_in"), sem("sel_in"), sem("c_in")
        wraw_in = per_layer(sem, "wraw_in")
        wa_in, wp_in = per_layer(sem, "wa_in"), per_layer(sem, "wp_in")
        zeroed, ident_ok, consts_ok, ones_ok = sem("zeroed"), sem("ident_ok"), sem("consts_ok"), sem("ones_ok")
        sel_ok, silu_ok = sem("sel_ok"), sem("silu_ok")
        w_lo = per_layer(sem, "w_lo")
        w_ok = per_layer(sem, "w_ok")
        ada_ps, ada_sb = per_layer(sem, "ada_ps"), per_layer(sem, "ada_sb")
        ada_one, ada_split = per_layer(sem, "ada_one"), per_layer(sem, "ada_split")
        mod_ok = per_layer(sem, "mod_ok")
        x_loaded, y_stored = sem("x_loaded"), sem("y_stored")
        mod_ps = per_layer(sem, "mod_ps")
        st_done = per_layer(sem, "st_done")
        aggr_begun = per_layer(sem, "aggr_begun")
        mv_done = per_layer(sem, "mv_done")
        veps_done = per_layer(sem, "veps_done")
        rstd_done = per_layer(sem, "rstd_done")
        t_done = per_layer(sem, "t_done")
        h_done = per_layer(sem, "h_done")
        hi_done = per_layer(sem, "hi_done")
        hcat_ok = per_layer(sem, "hcat_ok")
        hT_ps = per_layer(sem, "hT_ps")
        hT_sb = per_layer(sem, "hT_sb")
        v_ps, v_sb = per_layer(sem, "v_ps"), per_layer(sem, "v_sb")
        qk_ps = per_layer(sem, "qk_ps")
        qk_hi = per_layer(sem, "qk_hi")
        qk_ok = per_layer(sem, "qk_ok")
        s_ps = per_layer(sem, "s_ps")
        mx_ok = per_layer(sem, "mx_ok")
        mneg_ok = per_layer(sem, "mneg_ok")
        mT_ps, mT_sb = per_layer(sem, "mT_ps"), per_layer(sem, "mT_sb")
        m_moved = [[sem(f"m_moved{l}{b}") for b in range(2)] for l in range(2)]
        st_ps = per_layer(sem, "st_ps")
        exp_ok = per_layer(sem, "exp_ok")
        cut_begun = sem("cut_begun")
        cut_ok = sem("cut_ok")
        av_ps = per_layer(sem, "av_ps")
        o_sb = per_layer(sem, "o_sb")
        on_ps = per_layer(sem, "on_ps")
        rden_ok = per_layer(sem, "rden_ok")
        on_ok = per_layer(sem, "on_ok")
        onT_ps, onT_sb = per_layer(sem, "onT_ps"), per_layer(sem, "onT_sb")
        pj_ps = per_layer(sem, "pj_ps")
        gated_ok = per_layer(sem, "gated_ok")
        xmid_ok = per_layer(sem, "xmid_ok")
        f_ps, f_sb = per_layer(sem, "f_ps"), per_layer(sem, "f_sb")
        y_ps = per_layer(sem, "y_ps")
        xout_ok = per_layer(sem, "xout_ok")

        block = ctx.enter_context(nc.Block())

        STEPS = 19

        def turns(eng, step):
            for s in range(STEPS):
                step(s, 0, 0)
            for s in range(STEPS):
                step(s, 1, 0)
                step(s, 0, 1)
            with eng.Fori(2, PAIRS) as i:
                for s in range(STEPS):
                    step(s, 1, i - 1)
                    step(s, 0, i)
            for s in range(STEPS):
                step(s, 1, PAIRS - 1)

        @block.sync
        def _(sp):
            sp.dma_start(c_sb[:, :, :], c_rep).then_inc(c_in, 16)
            sp.dma_start(wmask_sb[:, :], wmask).then_inc(const_in, 16)
            sp.dma_start(qkmask_sb[:, :], qkmask).then_inc(const_in, 16)
            sp.dma_start(selc[:, :], batch_sel).then_inc(sel_in, 16)
            for l in range(2):
                sp.dma_start(wa_sb[l][:, :, :], w_ada[l]).then_inc(wa_in[l], 16)
                sp.dma_start(w_raw[l][:, :, :], w_cat[l]).then_inc(wraw_in[l], 16)
                sp.dma_start(wp_sb[l][:, :, :], w_proj[l]).then_inc(wp_in[l], 16)
                sp.dma_start(w2_sb[l][:, :, :], w_fc2[l]).then_inc(wp_in[l], 16)

            def step(s, l, it):
                if s in (7, 8):
                    b = s - 7
                    sp.wait_ge(mT_sb[l], at(it, 2, b + 1))
                    sp.dma_start(qkT[l][MROW:128:SLOT, 0:NG, b * T:(b + 1) * T],
                                 mrow[l][b][:, :, :]).then_inc(m_moved[l][b], 16)
                if s == 18 and l == 1:
                    sp.wait_ge(xout_ok[1], at(it, 1, 1))
                    sp.dma_start(out[bass.ds(2 * it, 2), :, :].rearrange("b t d -> t b d"),
                                 x_fin[:, :, :]).then_inc(y_stored, 16)

            turns(sp, step)
            sp.wait_ge(y_stored, 16 * PAIRS)

        @block.gpsimd
        def _(pool):
            nc.gpsimd.memset(ident[:, :], 0.0).then_inc(zeroed, 1)
            nc.gpsimd.memset(causal[:, :, :], 0.0).then_inc(zeroed, 1)
            nc.gpsimd.memset(minus_half[:, :], -0.5).then_inc(zeroed, 1)
            nc.gpsimd.memset(eps_sb[:, :], EPS).then_inc(zeroed, 1)
            pool.wait_ge(zeroed, 4)
            nc.gpsimd.affine_select(out=ident[:, :], in_=ident[:, :], compare_op=ALU.not_equal, fill=1.0,
                                    base=0, pattern=[[-1, 128]], channel_multiplier=1).then_inc(ident_ok, 1)
            nc.gpsimd.affine_select(out=causal[:, :, :], in_=causal[:, :, :], compare_op=ALU.is_ge, fill=-1e30,
                                    base=0, pattern=[[0, NG], [-1, 128]], channel_multiplier=1).then_inc(ident_ok, 1)

            def step(s, l, it):
                if s == 0 and l == 0:
                    wait(pool, xmid_ok[0], at(it, 1, 0))
                    pool.dma_start(x_in[0][:, :, :],
                                   x[bass.ds(2 * it, 2), :, :].rearrange("b t d -> t b d")).then_inc(x_loaded, 16)
                if s in (0, 15):
                    n = 0 if s == 0 else 1
                    pool.wait_ge(mv_done[l], at(it, 4, 2 * n + 2))
                    nc.gpsimd.tensor_tensor(veps[l][:, :], mv[l][:, :, 1], eps_sb[:, :], ALU.add).then_inc(veps_done[l], 1)
                    pool.wait_ge(veps_done[l], at(it, 2, n + 1))
                    nc.gpsimd.tensor_tensor(rstd[l][:, :], veps[l][:, :], minus_half[:, :], ALU.pow).then_inc(rstd_done[l], 1)
                if 8 <= s < 12 and l == 0:
                    u = s - 8
                    pool.wait_ge(exp_ok[0], at(it, 4, u + 1))
                    pool.sem_inc(cut_begun, 1)
                    p = probs[0][u % 2][:, :, :, :].rearrange("k j g q -> k (j g) q")
                    nc.gpsimd.affine_select(out=p, in_=p, compare_op=ALU.is_ge, fill=0.0, base=0,
                                            pattern=[[0, 2 * NG], [1, 128]],
                                            channel_multiplier=-1).then_inc(cut_ok, 1)

            turns(pool, step)

        @block.scalar
        def _(act):
            act.wait_ge(c_in, 16)
            act.wait_ge(ones_ok, 1)
            nc.scalar.activation(sc_sb[0:HALF, :, :], c_sb[0:HALF, :, :], ACT.Silu).then_inc(silu_ok, 1)
            act.wait_ge(ident_ok, 2)
            nc.scalar.copy(ident16[:, :], ident[:, :]).then_inc(consts_ok, 1)
            nc.scalar.copy(identb[:, :], ident[:, :]).then_inc(consts_ok, 1)
            act.wait_ge(const_in, 32)
            for l in range(2):
                act.wait_ge(ada_ps[l], 1)
                nc.scalar.copy(mod_f[l][:, :].rearrange("p (a n) -> p a n", a=2),
                               ps[l][0:MREP, 0:2, 0:MOD // 2]).then_inc(ada_sb[l], 1)
                act.wait_ge(wraw_in[l], 16)
                for k in range(CH):
                    if CH * l + k > 0:
                        act.wait_ge(w_ok[(CH * l + k - 1) // CH], (CH * l + k - 1) % CH + 1)
                    nc.scalar.activation(w_t[:, :], w_raw[l][:, k, :], ACT.Copy,
                                         scale=wmask_sb[:, k:k + 1]).then_inc(w_lo[l], 1)

            def step(s, l, it):
                if s in (1, 16):
                    n = 0 if s == 1 else 1
                    bank = 2 if n == 0 else 0
                    act.wait_ge(hT_ps[l], at(it, 2, n + 1))
                    if n == 0:
                        wait(act, f_ps[l], at(it, 3, 0))
                    else:
                        act.wait_ge(qk_ps[l], at(it, 4, 4))
                        act.wait_ge(v_ps[l], at(it, 1, 1))
                    nc.scalar.copy(hT[l][:, :, :],
                                   ps[l][0:KR, bank, :].bitcast(F16).rearrange("p (c t) -> p c t", c=CH)
                                   ).then_inc(hT_sb[l], 1)
                if s == 2:
                    act.wait_ge(v_ps[l], at(it, 1, 1))
                    wait(act, av_ps[l], at(it, 4, 0))
                    nc.scalar.activation(v_aug[l][:, :, :, 0:HD],
                                         ps[l][:, 3, 0:2 * D].rearrange("p (b h d) -> p b h d", b=2, h=H),
                                         ACT.Copy, scale=1.0 / WS).then_inc(v_sb[l], 1)
                if s in (2, 3):
                    for gp in (0, 1) if s == 2 else (2, 3):
                        act.wait_ge(qk_ps[l], at(it, 4, gp + 1))
                        wait(act, qk_ok[l], at(it, 4, 0))
                        nc.scalar.activation(qk_lo[l][:, gp, :], ps[l][:, gp, :], ACT.Copy,
                                             scale=qkmask_sb[:, gp // 2:gp // 2 + 1]).then_inc(qk_hi[l], 1)
                if s in (7, 8):
                    b = s - 7
                    act.wait_ge(mT_ps[l], at(it, 2, b + 1))
                    wait(act, m_moved[l][b], at(it, 16, 0))
                    nc.scalar.copy(mrow[l][b][:, :, :],
                                   ps[l][0:NJ, 2 + b, 0:256].bitcast(F16).rearrange("p (g q) -> p g q", g=NG)
                                   ).then_inc(mT_sb[l], 1)
                if 8 <= s < 12:
                    u = s - 8
                    act.wait_ge(st_ps[l], at(it, 4, u + 1))
                    wait(act, av_ps[l], at(it, 4, max(u - 1, 0)))
                    nc.scalar.activation(probs[l][u % 2][:, :, :, :],
                                         ps[l][:, 0:2, :].rearrange("p j (g q) -> p j g q", g=NG),
                                         ACT.Exp, scale=float(HD) ** -0.5).then_inc(exp_ok[l], 1)
                if s in (10, 12):
                    b = 0 if s == 10 else 1
                    act.wait_ge(av_ps[l], at(it, 4, 2 * b + 2))
                    wait(act, on_ps[l], at(it, 2, b))
                    nc.scalar.copy(oT[l][:, :, :],
                                   ps[l][:, 2, :].rearrange("p (g q) -> p g q", g=NG)).then_inc(o_sb[l], 1)
                if s in (12, 14):
                    b = 0 if s == 12 else 1
                    act.wait_ge(onT_ps[l], at(it, 2, b + 1))
                    wait(act, pj_ps[l], at(it, 1, 0))
                    nc.scalar.copy(onT[l][:, b, :, :],
                                   ps[l][0:HALF + 1, 3 - b, 0:256].rearrange("p (c q) -> p c q", c=2)
                                   ).then_inc(onT_sb[l], 1)
                if s == 17:
                    func = ACT.Silu if l == 0 else ACT.Gelu_apprx_tanh
                    wait(act, y_ps[l], at(it, 1, 0))
                    for k in range(3):
                        act.wait_ge(f_ps[l], at(it, 3, k + 1))
                        if k < 2:
                            o = ffT[l][:, 2 * k:2 * k + 2, :]
                            i = ps[l][:, 1 + k, :].rearrange("p (c t) -> p c t", c=2)
                        else:
                            o = ffT[l][0:FLAST, FCH - 1, :]
                            i = ps[l][0:FLAST, 3, 0:TOK]
                        nc.scalar.activation(o, i, func, scale=1.0 / WS).then_inc(f_sb[l], 1)

            turns(act, step)

        @block.vector
        def _(dve):
            nc.vector.memset(sc_sb[:, :, :], 1.0).then_inc(ones_ok, 1)
            for l in range(2):
                nc.vector.memset(h_cat[l][:, :, 3 * D:CAT], 1.0).then_inc(ones_ok, 1)
                nc.vector.memset(v_aug[l][:, :, :, HD], 1.0).then_inc(ones_ok, 1)
                nc.vector.memset(o_nat[l][:, :, :, HALF], 1.0).then_inc(ones_ok, 1)
                nc.vector.memset(ffT[l][64:128, FCH - 1, :], 1.0).then_inc(ones_ok, 1)
            dve.wait_ge(sel_in, 16)
            nc.vector.tensor_copy(sel[:, :, :], selc[:, :].unsqueeze(2).broadcast_to([MREP, B, 128])).then_inc(sel_ok, 1)
            dve.wait_ge(const_in, 32)

            def modulation(l):
                f, r, p = mod_f[l], mod_r, mod_b[l]
                if l == 1:
                    dve.wait_ge(mod_ok[0], 1)
                dve.wait_ge(ada_sb[l], 1)
                scales = f[:, :].rearrange("p (a s n) -> p a s n", a=2, s=3)[:, :, 1, :]
                nc.vector.tensor_scalar(scales, scales, 1.0, None, ALU.add).then_inc(ada_one[l], 1)
                dve.wait_ge(ada_one[l], 1)
                nc.vector.tensor_copy(p[:, :], f[:, :]).then_inc(ada_split[l], 1)
                dve.wait_ge(ada_split[l], 1)
                for q in (32, 64):
                    nc.vector.tensor_tensor(r[q:q + 32, :], f[q:q + 32, :], p[q:q + 32, :],
                                            ALU.subtract).then_inc(ada_split[l], 1)
                dve.wait_ge(ada_split[l], 3)
                for q in (32, 64):
                    nc.vector.tensor_copy(p[q:q + 32, :], r[q:q + 32, :]).then_inc(ada_split[l], 1)
                dve.wait_ge(ada_split[l], 5)
                nc.vector.tensor_tensor(f[64:96, :], r[64:96, :], p[64:96, :],
                                        ALU.subtract).then_inc(ada_split[l], 1)
                dve.wait_ge(ada_split[l], 6)
                nc.vector.tensor_copy(p[64:96, :], f[64:96, :]).then_inc(mod_ok[l], 1)

            for l in range(2):
                modulation(l)
                for k in range(CH):
                    dve.wait_ge(w_lo[l], k + 1)
                    nc.vector.scalar_tensor_tensor(out=w16[l][:, k, :], in0=w_raw[l][:, k, :], scalar=WS,
                                                   in1=w_t[:, :], op0=ALU.mult, op1=ALU.subtract).then_inc(w_ok[l], 1)

            def layer_norm(l, it, n, x_sb, mod_at):
                for b in range(2):
                    nc.vector.bn_stats(out=stats[l][:, b, :], in_=x_sb[:, b, :]).then_inc(st_done[l], 1)
                dve.wait_ge(st_done[l], at(it, 4, 2 * n + 2))
                dve.sem_inc(aggr_begun[l], 1)
                for b in range(2):
                    nc.vector.bn_aggr(out=mv[l][:, b, :], in_=stats[l][:, b, :]).then_inc(mv_done[l], 1)
                dve.wait_ge(mv_done[l], at(it, 4, 2 * n + 2))
                dve.wait_ge(mod_ps[l], at(it, 2, n + 1))
                for b in range(2):
                    nc.vector.scalar_tensor_tensor(out=ln_t[l][:, b, :], in0=x_sb[:, b, :], scalar=mv[l][:, b, 0:1],
                                                   in1=mod_at(b)[:, D:2 * D], op0=ALU.subtract,
                                                   op1=ALU.mult).then_inc(t_done[l], 1)
                dve.wait_ge(rstd_done[l], at(it, 2, n + 1))
                for b in range(2):
                    dve.wait_ge(t_done[l], at(it, 4, 2 * n + b + 1))
                    nc.vector.scalar_tensor_tensor(out=ln_h[l][:, b, :], in0=ln_t[l][:, b, :],
                                                   scalar=rstd[l][:, b:b + 1], in1=mod_at(b)[:, 0:D],
                                                   op0=ALU.mult, op1=ALU.add).then_inc(h_done[l], 1)
                dve.wait_ge(h_done[l], at(it, 4, 2 * n + 2))
                wait(dve, hT_ps[l], at(it, 2, n))
                for k in range(2):
                    nc.vector.tensor_copy(h_cat[l][:, :, k * D:(k + 1) * D], ln_h[l][:, :, :]).then_inc(hi_done[l], 1)
                dve.wait_ge(hi_done[l], at(it, 4, 2 * n + 2))
                nc.vector.tensor_tensor(h_cat[l][:, :, 2 * D:3 * D], ln_h[l][:, :, :], h_cat[l][:, :, 0:D],
                                        ALU.subtract).then_inc(hcat_ok[l], 1)

            def residual(l, it, n, x_sb, x_out, done):
                nc.vector.tensor_copy(gated[l][:, :, :],
                                      ps[l][:, 1, 0:2 * D].rearrange("p (b d) -> p b d", b=2)).then_inc(gated_ok[l], 1)
                dve.wait_ge(gated_ok[l], at(it, 4, 2 * n + 1))
                nc.vector.tensor_tensor(gated[l][:, :, :], ps[l][:, 0, 0:2 * D].rearrange("p (b d) -> p b d", b=2),
                                        gated[l][:, :, :], ALU.mult).then_inc(gated_ok[l], 1)
                dve.wait_ge(gated_ok[l], at(it, 4, 2 * n + 2))
                nc.vector.tensor_tensor(x_out[:, :, :], x_sb[:, :, :], gated[l][:, :, :], ALU.add).then_inc(done, 1)

            def step(s, l, it):
                if s == 0:
                    if l == 0:
                        dve.wait_ge(x_loaded, at(it, 16, 16))
                    else:
                        dve.wait_ge(xout_ok[0], at(it, 1, 1))
                    layer_norm(l, it, 0, x_in[l], lambda b: ps[l][:, b, :])
                if s in (2, 3):
                    for gp in (0, 1) if s == 2 else (2, 3):
                        dve.wait_ge(qk_hi[l], at(it, 4, gp + 1))
                        wait(dve, st_ps[l], at(it, 4, 0))
                        nc.vector.scalar_tensor_tensor(
                            out=qkT[l][:, 2 * gp:2 * gp + 2, :].rearrange("p g t -> p (g t)"),
                            in0=ps[l][:, gp, :], scalar=1.0 / WS, in1=qk_lo[l][:, gp, :],
                            op0=ALU.mult, op1=ALU.subtract).then_inc(qk_ok[l], 1)
                if 4 <= s < 8:
                    u = s - 4
                    b, half = u // 2, u % 2
                    dve.wait_ge(s_ps[l], at(it, 4, u + 1))
                    nc.vector.tensor_reduce(mx[l][:, b, 2 * half:2 * half + 2, :],
                                            ps[l][:, 0:2, :].rearrange("p j (g k) -> p j g k", g=NG),
                                            AX_X, ALU.max).then_inc(mx_ok[l], 1)
                    if half == 1:
                        dve.wait_ge(mx_ok[l], at(it, 4, u + 1))
                        wait(dve, mT_ps[l], at(it, 2, 0))
                        nc.vector.tensor_scalar(mneg[l][:, b, :, :], mx[l][:, b, :, :].rearrange("p j g -> p g j"),
                                                -1.0 / MS, None, ALU.mult).then_inc(mneg_ok[l], 1)
                if s in (11, 13):
                    b = 0 if s == 11 else 1
                    dve.wait_ge(on_ps[l], at(it, 2, b + 1))
                    heads = ps[l][:, 3 - b, :].rearrange("p (h s) -> p h s", h=H)
                    nc.vector.reciprocal(out=rden[l][:, b, :], in_=heads[:, :, HD]).then_inc(rden_ok[l], 1)
                    dve.wait_ge(rden_ok[l], at(it, 2, b + 1))
                    wait(dve, onT_ps[l], at(it, 2, 0))
                    for c in range(2):
                        hs = slice(c * H // 2, (c + 1) * H // 2)
                        nc.vector.tensor_tensor(
                            o_nat[l][:, b, c, 0:HALF].rearrange("p (h d) -> p h d", d=HD), heads[:, hs, 0:HD],
                            rden[l][:, b, hs].unsqueeze(2).broadcast_to([128, H // 2, HD]),
                            ALU.mult).then_inc(on_ok[l], 1)
                if s == 15:
                    dve.wait_ge(pj_ps[l], at(it, 1, 1))
                    residual(l, it, 0, x_in[l], x_mid[l], xmid_ok[l])
                    dve.wait_ge(xmid_ok[l], at(it, 1, 1))
                    layer_norm(l, it, 1, x_mid[l], lambda b: ps[l][:, 2 + b, :])
                if s == 18:
                    dve.wait_ge(y_ps[l], at(it, 1, 1))
                    if l == 0:
                        wait(dve, xmid_ok[1], at(it, 1, 0))
                        residual(l, it, 1, x_mid[l], x_in[1], xout_ok[0])
                    else:
                        wait(dve, y_stored, at(it, 16, 0))
                        residual(l, it, 1, x_mid[l], x_fin, xout_ok[1])

            turns(dve, step)

        @block.tensor
        def _(pe):
            pe.wait_ge(silu_ok, 1)
            for l in range(2):
                pe.wait_ge(wa_in[l], 16)
                for n in range(2):
                    for c in range(2):
                        last = nc.tensor.matmul(ps[l][0:MREP, n, 0:MOD // 2], sc_sb[:, c, :],
                                                wa_sb[l][:, c, n * MOD // 2:(n + 1) * MOD // 2],
                                                start=(c == 0), stop=(c == 1))
                last.then_inc(ada_ps[l], 1)
            pe.wait_ge(sel_ok, 1)
            pe.wait_ge(consts_ok, 2)
            pe.wait_ge(ones_ok, 9)

            def modulation(l, it, at_b, cols):
                for b in range(2):
                    n = cols.stop - cols.start
                    last = nc.tensor.matmul(at_b(b), sel[:, bass.ds(2 * it + b, 1), :].rearrange("p a t -> p (a t)"),
                                            mod_b[l][:, cols], start=True, stop=True)
                return last

            def transpose_h(l, bank):
                dst = ps[l][0:KR, bank, :].bitcast(F16).rearrange("p (c t) -> p c t", c=CH)
                for b in range(2):
                    for c in range(CH):
                        last = nc.tensor.transpose(dst[:, c, b * T:(b + 1) * T],
                                                   h_cat[l][:, b, c * KR:(c + 1) * KR], ident16[:, :])
                return last

            def stacked(out, l, cols):
                for c in range(CH):
                    last = nc.tensor.matmul(out, w16[l][:, c, cols], hT[l][:, c, :], start=(c == 0), stop=(c == CH - 1))
                return last

            def q_and_k(l, gp):
                for n in range(2):
                    g = 2 * gp + n
                    last = stacked(ps[l][:, gp, n * TOK:(n + 1) * TOK], l, slice(g * 128, (g + 1) * 128))
                last.then_inc(qk_ps[l], 1)

            def scores(l, u):
                b, half = u // 2, u % 2
                ts = slice(b * T, (b + 1) * T)
                if l == 0:
                    for jj in range(2):
                        nc.tensor.matmul(ps[0][:, jj, :], identb[:, :], causal[:, :, :], start=True, stop=False,
                                         skip_group_check=True)
                for g in range(NG):
                    for jj in range(2):
                        r = SLOT * (2 * half + jj)
                        last = nc.tensor.matmul(ps[l][:, jj, g * 128:(g + 1) * 128], qkT[l][r:r + PARTS, g, ts],
                                                qkT[l][r:r + PARTS, NG + g, ts], start=(l == 1), stop=True,
                                                skip_group_check=True)
                last.then_inc(s_ps[l], 1)

            def scores_by_key(l, u):
                b, half = u // 2, u % 2
                ts = slice(b * T, (b + 1) * T)
                for g in range(NG):
                    for jj in range(2):
                        r = SLOT * (2 * half + jj)
                        last = nc.tensor.matmul(ps[l][:, jj, g * 128:(g + 1) * 128], qkT[l][r:r + PARTS + 1, NG + g, ts],
                                                qkT[l][r:r + PARTS + 1, g, ts], start=True, stop=True,
                                                skip_group_check=True)
                last.then_inc(st_ps[l], 1)

            def values(l, u):
                b, half = u // 2, u % 2
                for g in range(NG):
                    for jj in range(2):
                        j = 2 * half + jj
                        last = nc.tensor.matmul(ps[l][SLOT * j:SLOT * j + HD + 1, 2, g * 128:(g + 1) * 128],
                                                v_aug[l][:, b, NJ * g + j, :], probs[l][u % 2][:, jj, g, :],
                                                start=True, stop=True, skip_group_check=True)
                last.then_inc(av_ps[l], 1)

            def maxima(l, b):
                dst = ps[l][0:NJ, 2 + b, 0:256].bitcast(F16).rearrange("p (g q) -> p g q", g=NG)
                for g in range(NG):
                    last = nc.tensor.transpose(dst[:, g, :], mneg[l][:, b, g, :], ident16[:, :])
                last.then_inc(mT_ps[l], 1)

            def by_query(l, b):
                for g in range(NG):
                    last = nc.tensor.transpose(ps[l][:, 3 - b, g * 128:(g + 1) * 128], oT[l][:, g, :], ident[:, :])
                last.then_inc(on_ps[l], 1)

            def by_channel(l, b):
                for c in range(2):
                    last = nc.tensor.transpose(ps[l][0:HALF + 1, 3 - b, c * 128:(c + 1) * 128],
                                               o_nat[l][:, b, c, :], ident[:, :])
                last.then_inc(onT_ps[l], 1)

            def values_ready(l, it, u):
                if l == 0:
                    pe.wait_ge(cut_ok, at(it, 4, u + 1))
                else:
                    pe.wait_ge(exp_ok[1], at(it, 4, u + 1))

            def step(s, l, it):
                if s == 0:
                    if isinstance(it, int) and it == 0 or l == 1:
                        pe.wait_ge(mod_ok[l], 1)
                    wait(pe, xout_ok[l], at(it, 1, 0))
                    modulation(l, it, lambda b: ps[l][:, b, 0:2 * D], slice(0, 2 * D)).then_inc(mod_ps[l], 1)
                if s == 1:
                    pe.wait_ge(hcat_ok[l], at(it, 2, 1))
                    transpose_h(l, 2).then_inc(hT_ps[l], 1)
                if s == 2:
                    pe.wait_ge(hT_sb[l], at(it, 2, 1))
                    pe.wait_ge(w_ok[l], CH)
                    for b in range(2):
                        for c in range(CH):
                            last = nc.tensor.matmul(ps[l][:, 3, b * D:(b + 1) * D], hT[l][:, c, b * T:(b + 1) * T],
                                                    w16[l][:, c, QK:QK + D], start=(c == 0), stop=(c == CH - 1))
                    last.then_inc(v_ps[l], 1)
                    q_and_k(l, 0)
                    q_and_k(l, 1)
                if s == 3:
                    q_and_k(l, 2)
                    pe.wait_ge(v_sb[l], at(it, 1, 1))
                    q_and_k(l, 3)
                if s == 4:
                    pe.wait_ge(qk_ok[l], at(it, 4, 4))
                    scores(l, 0)
                if s == 5:
                    pe.wait_ge(mx_ok[l], at(it, 4, 1))
                    scores(l, 1)
                if s == 6:
                    pe.wait_ge(mx_ok[l], at(it, 4, 2))
                    scores(l, 2)
                    pe.wait_ge(mneg_ok[l], at(it, 2, 1))
                    maxima(l, 0)
                if s == 7:
                    pe.wait_ge(mx_ok[l], at(it, 4, 3))
                    scores(l, 3)
                if s == 8:
                    pe.wait_ge(mneg_ok[l], at(it, 2, 2))
                    maxima(l, 1)
                    pe.wait_ge(m_moved[l][0], at(it, 16, 16))
                    scores_by_key(l, 0)
                if s == 9:
                    pe.wait_ge(exp_ok[l], at(it, 4, 1))
                    scores_by_key(l, 1)
                    values_ready(l, it, 0)
                    pe.wait_ge(mT_sb[l], at(it, 2, 1))
                    values(l, 0)
                if s == 10:
                    pe.wait_ge(exp_ok[l], at(it, 4, 2))
                    pe.wait_ge(m_moved[l][1], at(it, 16, 16))
                    scores_by_key(l, 2)
                    values_ready(l, it, 1)
                    values(l, 1)
                if s == 11:
                    pe.wait_ge(exp_ok[l], at(it, 4, 3))
                    scores_by_key(l, 3)
                    pe.wait_ge(o_sb[l], at(it, 2, 1))
                    pe.wait_ge(mT_sb[l], at(it, 2, 2))
                    by_query(l, 0)
                    values_ready(l, it, 2)
                    values(l, 2)
                if s == 12:
                    pe.wait_ge(on_ok[l], at(it, 4, 2))
                    by_channel(l, 0)
                    values_ready(l, it, 3)
                    values(l, 3)
                if s == 13:
                    pe.wait_ge(o_sb[l], at(it, 2, 2))
                    by_query(l, 1)
                    pe.wait_ge(exp_ok[l], at(it, 4, 4))
                    modulation(l, it, lambda b: ps[l][:, 1, b * D:(b + 1) * D], slice(2 * D, 3 * D))
                if s == 14:
                    pe.wait_ge(on_ok[l], at(it, 4, 4))
                    by_channel(l, 1)
                if s == 15:
                    pe.wait_ge(onT_sb[l], at(it, 2, 2))
                    pe.wait_ge(wp_in[l], 32)
                    for b in range(2):
                        for c in range(2):
                            k = HALF + 1 - c
                            last = nc.tensor.matmul(ps[l][:, 0, b * D:(b + 1) * D], onT[l][0:k, b, c, :],
                                                    wp_sb[l][0:k, c, :], start=(c == 0), stop=(c == 1))
                    last.then_inc(pj_ps[l], 1)
                    modulation(l, it, lambda b: ps[l][:, 2 + b, 0:2 * D], slice(3 * D, 5 * D)).then_inc(mod_ps[l], 1)
                if s == 16:
                    pe.wait_ge(hcat_ok[l], at(it, 2, 2))
                    transpose_h(l, 0).then_inc(hT_ps[l], 1)
                if s == 17:
                    pe.wait_ge(hT_sb[l], at(it, 2, 2))
                    for m in range(FCH):
                        rows = 128 if m < FCH - 1 else FLAST
                        w0 = QK + D + 128 * m
                        last = stacked(ps[l][0:rows, 1 + m // 2, (m % 2) * TOK:(m % 2 + 1) * TOK], l,
                                       slice(w0, w0 + rows))
                        if m % 2 == 1 or m == FCH - 1:
                            last.then_inc(f_ps[l], 1)
                if s == 18:
                    pe.wait_ge(f_sb[l], at(it, 3, 1))
                    modulation(l, it, lambda b: ps[l][:, 1, b * D:(b + 1) * D], slice(5 * D, 6 * D))
                    pe.wait_ge(f_sb[l], at(it, 3, 3))
                    for b in range(2):
                        for m in range(FCH):
                            rows = 128 if m < FCH - 1 else FLAST + 1
                            last = nc.tensor.matmul(ps[l][:, 0, b * D:(b + 1) * D], ffT[l][0:rows, m, b * T:(b + 1) * T],
                                                    w2_sb[l][0:rows, m, :], start=(m == 0), stop=(m == FCH - 1))
                    last.then_inc(y_ps[l], 1)

            turns(pe, step)


def _layout(inputs):
    import numpy as np

    f = {k: np.asarray(v) for k, v in inputs.items()}

    def slots(w, third):
        w = w.reshape(-1, NG, NJ, HD)
        o = np.zeros((w.shape[0], NG, NJ, SLOT), w.dtype)
        for p in range(3):
            o[..., p * HD:(p + 1) * HD] = w
        o[..., MROW] = third
        return o.reshape(w.shape[0], -1)

    def cat(wq, wk, wv, w1, bq, bk, bv, b1):
        w = np.concatenate([slots(wq, 0), slots(wk, 0), wv, w1], axis=1)
        hi = np.concatenate([slots(bq[None], 0), slots(bk[None], MS), bv[None], b1[None]], axis=1)
        lo = np.concatenate([slots(bq[None], 0), slots(bk[None], MS), bv[None], b1[None]], axis=1)
        rows = np.concatenate([w, w, w, hi, lo, np.zeros((CAT - 3 * D - 2, WCOLS), w.dtype)], axis=0)
        return np.ascontiguousarray(rows.reshape(CH, KR, WCOLS).transpose(1, 0, 2))

    def halves(w, bias):
        o = np.zeros((HALF + 1, 2, w.shape[1]), w.dtype)
        o[:HALF] = w.reshape(2, HALF, -1).transpose(1, 0, 2)
        o[HALF, 0] = bias
        return o

    def hidden(w, bias):
        o = np.zeros((FCH * 128, w.shape[1]), w.dtype)
        o[:FF] = w
        o[FF] = bias
        return np.ascontiguousarray(o.reshape(FCH, 128, -1).transpose(1, 0, 2))

    z = np.zeros(D, np.float32)
    wq, wk, wv = np.split(f["L1_cond_W_qkv"], 3, axis=1)
    bq, bk, bv = np.split(f["L1_cond_b_qkv"], 3)
    a = {"x": f["x"]}
    a["w_cat0"] = cat(f["L0_cond_Wq"], f["L0_cond_Wk"], f["L0_cond_Wv"], f["L0_cond_W1"], z, z, z, f["L0_cond_b1"])
    a["w_cat1"] = cat(wq, wk, wv, f["L1_cond_W_fc1"], bq, bk, bv, f["L1_cond_b_fc1"])
    a["w_proj0"] = halves(f["L0_cond_Wp"], f["L0_cond_bp"])
    a["w_proj1"] = halves(f["L1_cond_W_proj"], f["L1_cond_b_proj"])
    a["w_fc2_0"] = hidden(f["L0_cond_W2"], f["L0_cond_b2"])
    a["w_fc2_1"] = hidden(f["L1_cond_W_fc2"], f["L1_cond_b_fc2"])
    a["w_ada0"] = halves(f["L0_cond_Wa"], f["L0_cond_ba"])
    a["w_ada1"] = halves(f["L1_cond_W_ada"], f["L1_cond_b_ada"])
    c = f["cond_1152"]
    c_rep = np.zeros((HALF + 1, 2, MREP), c.dtype)
    for p in range(3):
        c_rep[:HALF, :, 32 * p:32 * p + B] = c.T.reshape(2, HALF, B).transpose(1, 0, 2)
    a["c_rep"] = c_rep
    r = np.arange(CAT).reshape(CH, KR).T
    low = ((r >= D) & (r < 2 * D)) | (r == 3 * D + 1)
    a["wmask"] = np.ascontiguousarray(np.where(low, WS, 0.0).astype(np.float32))
    slot = np.arange(128) % SLOT
    q_low = (slot >= 2 * HD) & (slot < 3 * HD)
    k_low = (slot >= HD) & (slot < 2 * HD)
    a["qkmask"] = np.stack([np.where(q_low, 1 / WS, 0.0), np.where(k_low, 1 / WS, 0.0)], axis=1).astype(np.float32)
    a["batch_sel"] = (np.arange(MREP)[:, None] % 32 == np.arange(B)[None]).astype(np.float32)
    return a


def kernel(**inputs):
    import concourse.bacc as bacc
    import numpy as np
    from concourse.bass_utils import run_bass_kernel_spmd

    nc = bacc.Bacc("TRN2", target_bir_lowering=False, num_devices=1)
    arrays = _layout(inputs)
    ap = {n: nc.dram_tensor(n + "_dram", a.shape, mybir.dt.from_np(a.dtype), kind="ExternalInput").ap()
          for n, a in arrays.items()}
    out = nc.dram_tensor("out_dram", (B, T, D), F32, kind="ExternalOutput").ap()
    two_layer_kernel(nc, ap["x"], ap["c_rep"], [ap["w_cat0"], ap["w_cat1"]], [ap["w_proj0"], ap["w_proj1"]],
                     [ap["w_fc2_0"], ap["w_fc2_1"]], [ap["w_ada0"], ap["w_ada1"]], ap["wmask"], ap["qkmask"],
                     ap["batch_sel"], out)
    r = run_bass_kernel_spmd(nc, [{n + "_dram": a for n, a in arrays.items()}], core_ids=[0])
    return np.asarray(r.results[0]["out_dram"])
```

```python
from contextlib import ExitStack

import concourse.bass as bass
from concourse import mybir

F32 = mybir.dt.float32
F16 = mybir.dt.float16
BF16 = mybir.dt.bfloat16
ALU = mybir.AluOpType
ACT = mybir.ActivationFunctionType
AX_X = mybir.AxisListType.X

B, T, D = 16, 128, 144
H = 16
HD = D // H
FF = 4 * D
EPS = 1e-6
PAIRS = B // 4
TOK = 2 * T

NJ, NG = 4, 4
SLOT = 128 // NJ
PARTS = 3 * HD
MROW = PARTS + 1
MS = 64.0

UNITS = 2 * NJ
NPROB = 4

CH = 4
KR = 109
CAT = CH * KR
QK = 2 * NG * 128
WCOLS = QK + D + FF
RAWCOLS = 3 * D + FF
BIAS_ROW = (3 * D) % KR
WS = 16.0
HALF = D // 2
FCH = (FF + 127) // 128
FLAST = FF - 128 * (FCH - 1)
MOD = 6 * D
MREP = 96


WAY = [("norm_stats", 0, -2.0), ("norm_rows", 0, -1.9), ("norm_parts", 0, -0.0), ("turn_h", 0, 1.7),
       ("v", 0, 2.5), ("qk", 0, 4.2), ("qk", 1, 4.9), ("qk", 2, 5.1), ("qk", 3, 5.6), ("score", 0, 9.8),
       ("score", 1, 12.2), ("score", 2, 12.4), ("score", 3, 13.1), ("score", 4, 13.6), ("score", 5, 15.2),
       ("score", 6, 15.8), ("maxima", 0, 16.0), ("score", 7, 16.5), ("maxima", 1, 17.5), ("weight", 0, 18.3),
       ("weight", 1, 19.0), ("weight", 2, 20.7), ("weight", 3, 20.9), ("weight", 4, 21.3), ("value", 0, 21.8),
       ("weight", 5, 22.1), ("value", 1, 22.1), ("value", 2, 22.7), ("value", 3, 23.0),
       ("values_out", 0, 23.2), ("weight", 6, 23.3), ("weight", 7, 23.4), ("value", 4, 24.0),
       ("value", 5, 24.5), ("by_query", 0, 24.6), ("value", 6, 24.7), ("value", 7, 25.0),
       ("values_out", 1, 25.2), ("by_query", 1, 25.8), ("by_channel", 0, 26.1), ("by_channel", 1, 27.9),
       ("project", 0, 28.8), ("norm_stats", 1, 32.7), ("norm_rows", 1, 34.0), ("norm_parts", 1, 34.2),
       ("turn_h", 1, 38.4), ("hidden", 0, 40.1), ("hidden", 1, 40.5), ("hidden", 2, 41.0),
       ("mlp_out", 0, 44.5)]
SPAN = 47.7
FIRST = ([("weights", 4 + i, 12.0 + 2.5 * i) for i in range(4)] + [("ada", 1, 8.0)]
         + [("weights", 8 + i, 23.0 + 2.0 * i) for i in range(8)])
LAG = 23.8


def first_row(stream, pair):
    return 2 * (PAIRS * stream + pair)


def at(pair, per_pair, k):
    return pair * per_pair + k


def wait(eng, sem, value):
    if not (isinstance(value, int) and value <= 0):
        eng.wait_ge(sem, value)


def two_layer_kernel(nc, x, c_rep, w_cat, w_proj, w_fc2, w_ada, wmask, qkmask, batch_sel, k_const, out):
    ctx = ExitStack()
    with ctx:
        def sb(name, shape, dt):
            return ctx.enter_context(nc.sbuf_tensor(name, shape, dt))

        def sem(name):
            return ctx.enter_context(nc.semaphore(name))

        def per_layer(make, name):
            return [make(f"{name}{l}") for l in range(2)]

        ident = sb("ident", [128, 128], F32)
        ident16 = sb("ident16", [128, 128], F16)
        identb = sb("identb", [128, 128], BF16)
        causal = sb("causal", [128, NG, 128], BF16)
        sel = sb("sel", [MREP, B, 128], F16)
        selc = sb("selc", [MREP, B], F32)
        wmask_sb = sb("wmask_sb", [KR, CH], F32)
        qkmask_sb = sb("qkmask_sb", [128, 2], F32)
        c_sb = sb("c_sb", [HALF + 1, 2, MREP], F32)
        sc_sb = sb("sc_sb", [HALF + 1, 2, MREP], F32)
        w_raw = [sb(f"w_raw{l}", [KR, CH, RAWCOLS], F32) for l in range(2)]
        w_t = sb("w_t", [KR, 2, FF], F16)
        x_all = sb("x_all", [128, B, D], F32)
        w16 = [sb(f"w16_{l}", [KR, CH, WCOLS], F16) for l in range(2)]
        wp_sb = [sb(f"wp_sb{l}", [HALF + 1, 2, D], F32) for l in range(2)]
        w2_sb = [sb(f"w2_sb{l}", [128, FCH, D], F32) for l in range(2)]
        wa_sb = [sb(f"wa_sb{l}", [HALF + 1, 2, MOD], F32) for l in range(2)]
        mod_f = [sb(f"mod_f{l}", [MREP, MOD], F32) for l in range(2)]
        mod_b = [sb(f"mod_b{l}", [MREP, MOD], F16) for l in range(2)]

        x_mid = [sb(f"x_mid{l}", [128, 2, D], F32) for l in range(2)]
        x_next = [sb(f"x_next{l}", [128, 2, D], F32) for l in range(2)]
        x_fin = [sb(f"x_fin{l}", [128, 2, D], F32) for l in range(2)]
        gated = [sb(f"gated{l}", [128, 2, D], F32) for l in range(2)]
        stats = [sb(f"stats{l}", [128, 2, 6], F32) for l in range(2)]
        mv = [sb(f"mv{l}", [128, 2, 2], F32) for l in range(2)]
        veps = [sb(f"veps{l}", [128, 2], F32) for l in range(2)]
        minus_half = sb("minus_half", [128, 2], F32)
        eps_sb = sb("eps_sb", [128, 2], F32)
        rstd = [sb(f"rstd{l}", [128, 2], F32) for l in range(2)]
        ln_t = [sb(f"ln_t{l}", [128, 2, D], F32) for l in range(2)]
        ln_h = [sb(f"ln_h{l}", [128, 2, D], F32) for l in range(2)]
        h_cat = [sb(f"h_cat{l}", [128, 2, CAT], F16) for l in range(2)]
        hT = [sb(f"hT{l}", [KR, CH, TOK], F16) for l in range(2)]
        v_aug = [sb(f"v_aug{l}", [128, 2, H, HD + 1], F32) for l in range(2)]
        qk_lo = [sb(f"qk_lo{l}", [128, 4, 2 * TOK], F16) for l in range(2)]
        qkT = [sb(f"qkT{l}", [128, 2 * NG, TOK], F16) for l in range(2)]
        mx = [sb(f"mx{l}", [128, 2, NJ, NG], F32) for l in range(2)]
        mneg = [sb(f"mneg{l}", [128, 2, NG, NJ], F16) for l in range(2)]
        mrow = [[sb(f"mrow{l}{b}", [NJ, NG, 128], F16) for b in range(2)] for l in range(2)]
        probs = [sb(f"probs{l}", [128, NPROB, NG, 128], F32) for l in range(2)]
        oT = [sb(f"oT{l}", [128, NG, 128], F32) for l in range(2)]
        rden = [sb(f"rden{l}", [128, 2, H], F32) for l in range(2)]
        o_nat = [sb(f"o_nat{l}", [128, 2, 2, HALF + 1], F32) for l in range(2)]
        onT = [sb(f"onT{l}", [HALF + 1, 2, 2, 128], F32) for l in range(2)]
        ffT = [sb(f"ffT{l}", [128, FCH, TOK], F32) for l in range(2)]
        ps = [ctx.enter_context(nc.psum_tensor(f"ps{l}", [128, 4, 512], F32)) for l in range(2)]

        const_in, sel_in, c_in = sem("const_in"), sem("sel_in"), sem("c_in")
        wraw_in = [[sem(f"wraw_in{l}{p}") for p in range(2)] for l in range(2)]
        kconst_in, spare_ok = sem("kconst_in"), sem("spare_ok")
        x_in = [sem(f"x_in{n}") for n in range(2)]
        wa_in, wp_in = per_layer(sem, "wa_in"), per_layer(sem, "wp_in")
        zeroed, ident_ok, consts_ok, ones_ok = sem("zeroed"), sem("ident_ok"), sem("consts_ok"), sem("ones_ok")
        sel_ok, silu_ok = sem("sel_ok"), sem("silu_ok")
        w_lo = sem("w_lo")
        w_ok = sem("w_ok")
        ada_ps, ada_sb = per_layer(sem, "ada_ps"), per_layer(sem, "ada_sb")
        ada_one, ada_split = per_layer(sem, "ada_one"), per_layer(sem, "ada_split")
        mod_ok = per_layer(sem, "mod_ok")
        y_stored = per_layer(sem, "y_stored")
        mod_ps = per_layer(sem, "mod_ps")
        st_done = per_layer(sem, "st_done")
        aggr_begun = per_layer(sem, "aggr_begun")
        mv_done = per_layer(sem, "mv_done")
        veps_done = per_layer(sem, "veps_done")
        rstd_done = per_layer(sem, "rstd_done")
        t_done = per_layer(sem, "t_done")
        h_done = per_layer(sem, "h_done")
        hi_done = per_layer(sem, "hi_done")
        hcat_ok = per_layer(sem, "hcat_ok")
        hT_ps = per_layer(sem, "hT_ps")
        hT_sb = per_layer(sem, "hT_sb")
        v_ps, v_sb = per_layer(sem, "v_ps"), per_layer(sem, "v_sb")
        qk_ps = per_layer(sem, "qk_ps")
        qk_hi = per_layer(sem, "qk_hi")
        qk_ok = per_layer(sem, "qk_ok")
        s_ps = per_layer(sem, "s_ps")
        mx_ok = per_layer(sem, "mx_ok")
        mneg_ok = per_layer(sem, "mneg_ok")
        mT_ps, mT_sb = per_layer(sem, "mT_ps"), per_layer(sem, "mT_sb")
        m_moved = [[sem(f"m_moved{l}{b}") for b in range(2)] for l in range(2)]
        st_ps = per_layer(sem, "st_ps")
        exp_ok = per_layer(sem, "exp_ok")
        cut_begun = per_layer(sem, "cut_begun")
        cut_ok = per_layer(sem, "cut_ok")
        av_ps = per_layer(sem, "av_ps")
        o_sb = per_layer(sem, "o_sb")
        on_ps = per_layer(sem, "on_ps")
        rden_ok = per_layer(sem, "rden_ok")
        on_ok = per_layer(sem, "on_ok")
        onT_ps, onT_sb = per_layer(sem, "onT_ps"), per_layer(sem, "onT_sb")
        pj_ps = per_layer(sem, "pj_ps")
        gated_ok = per_layer(sem, "gated_ok")
        xmid_ok = per_layer(sem, "xmid_ok")
        f_ps, f_sb = per_layer(sem, "f_ps"), per_layer(sem, "f_sb")
        y_ps = per_layer(sem, "y_ps")
        xout_ok = per_layer(sem, "xout_ok")

        block = ctx.enter_context(nc.Block())

        lead = [(t + l * SPAN, 0, l, name, k) for l in range(2) for name, k, t in WAY]
        follow = [(t + LAG, 1, l, name, k) for t, _, l, name, k in lead]
        within = sorted(lead + [e for e in follow if e[0] < 2 * SPAN])
        over = sorted((t - 2 * SPAN, st, l, name, k) for t, st, l, name, k in follow if t >= 2 * SPAN)

        def turns(eng, step, first=lambda name, k: None):
            for _, st, l, name, k in sorted(within + [(t, 2, 0, name, k) for name, k, t in FIRST]):
                if st == 2:
                    first(name, k)
                else:
                    step(name, k, l, st, 0, l)
            with eng.Fori(1, PAIRS) as i:
                for t, st, l, name, k in sorted(within + [(t, 2, l, name, k) for t, _, l, name, k in over]):
                    if st == 2:
                        step(name, k, l, 1, i - 1, 2 * (i - 1) + l)
                    else:
                        step(name, k, l, st, i, 2 * i + l)
            for _, st, l, name, k in over:
                step(name, k, l, st, PAIRS - 1, 2 * (PAIRS - 1) + l)

        @block.sync
        def _(sp):
            for st in range(2):
                sp.sem_inc(y_stored[st], 16)
            sp.dma_start(c_sb[:, :, :], c_rep).then_inc(c_in, 16)
            sp.dma_start(wa_sb[0][:, :, :], w_ada[0]).then_inc(wa_in[0], 16)
            sp.dma_start(selc[:, :], batch_sel).then_inc(sel_in, 16)
            sp.dma_start(wmask_sb[:, :], wmask).then_inc(const_in, 16)
            sp.dma_start(qkmask_sb[:, :], qkmask).then_inc(const_in, 16)
            sp.dma_start(w_raw[0][:, :, 0:3 * D], w_cat[0][:, :, 0:3 * D]).then_inc(wraw_in[0][0], 16)
            sp.dma_start(x_all[:, 0:2, :], x[0:2, :, :].rearrange("b t d -> t b d")).then_inc(x_in[0], 16)
            sp.wait_ge(spare_ok, 2)
            for l in range(2):
                slots = w16[l][BIAS_ROW:BIAS_ROW + 1, CH - 1, QK // 2:QK].rearrange("p (h s) -> p h s", s=SLOT)
                sp.dma_start(slots[:, :, MROW:MROW + 1], k_const,
                             allow_slow_non_contiguous=True).then_inc(kconst_in, 16)
            sp.dma_start(w_raw[0][:, :, 3 * D:RAWCOLS], w_cat[0][:, :, 3 * D:RAWCOLS]).then_inc(wraw_in[0][1], 16)
            sp.dma_start(x_all[:, 2:B, :], x[2:B, :, :].rearrange("b t d -> t b d")).then_inc(x_in[1], 16)
            sp.dma_start(wa_sb[1][:, :, :], w_ada[1]).then_inc(wa_in[1], 16)
            sp.dma_start(wp_sb[0][:, :, :], w_proj[0]).then_inc(wp_in[0], 16)
            sp.dma_start(w2_sb[0][:, :, :], w_fc2[0]).then_inc(wp_in[0], 16)
            sp.dma_start(w_raw[1][:, :, 0:3 * D], w_cat[1][:, :, 0:3 * D]).then_inc(wraw_in[1][0], 16)
            sp.dma_start(w_raw[1][:, :, 3 * D:RAWCOLS], w_cat[1][:, :, 3 * D:RAWCOLS]).then_inc(wraw_in[1][1], 16)
            sp.dma_start(wp_sb[1][:, :, :], w_proj[1]).then_inc(wp_in[1], 16)
            sp.dma_start(w2_sb[1][:, :, :], w_fc2[1]).then_inc(wp_in[1], 16)

            def step(stage, k, layer, st, it, turn):
                if stage == "maxima":
                    b = k
                    sp.wait_ge(mT_sb[st], at(turn, 2, b + 1))
                    sp.dma_start(qkT[st][MROW:128:SLOT, 0:NG, b * T:(b + 1) * T],
                                 mrow[st][b][:, :, :]).then_inc(m_moved[st][b], 16)
                if stage == "mlp_out" and layer == 1:
                    sp.wait_ge(xout_ok[st], at(turn, 1, 1))
                    sp.dma_start(out[bass.ds(first_row(st, it), 2), :, :].rearrange("b t d -> t b d"),
                                 x_fin[st][:, :, :]).then_inc(y_stored[st], 16)

            turns(sp, step)
            for st in range(2):
                sp.wait_ge(y_stored[st], at(PAIRS, 16, 16))

        @block.gpsimd
        def _(pool):
            nc.gpsimd.memset(ident[:, :], 0.0).then_inc(zeroed, 1)
            nc.gpsimd.memset(causal[:, :, :], 0.0).then_inc(zeroed, 1)
            nc.gpsimd.memset(minus_half[:, :], -0.5).then_inc(zeroed, 1)
            nc.gpsimd.memset(eps_sb[:, :], EPS).then_inc(zeroed, 1)
            for l in range(2):
                spare = w16[l][:, :, 0:QK].rearrange("p c (h s) -> p c h s", s=SLOT)[:, :, :, PARTS:SLOT]
                nc.gpsimd.memset(spare, 0.0).then_inc(spare_ok, 1)
            pool.wait_ge(zeroed, 4)
            nc.gpsimd.affine_select(out=ident[:, :], in_=ident[:, :], compare_op=ALU.not_equal, fill=1.0,
                                    base=0, pattern=[[-1, 128]], channel_multiplier=1).then_inc(ident_ok, 1)
            nc.gpsimd.affine_select(out=causal[:, :, :], in_=causal[:, :, :], compare_op=ALU.is_ge, fill=-1e30,
                                    base=0, pattern=[[0, NG], [-1, 128]], channel_multiplier=1).then_inc(ident_ok, 1)

            def step(stage, k, layer, st, it, turn):
                if stage == "norm_stats":
                    n = k
                    pool.wait_ge(mv_done[st], at(turn, 4, 2 * n + 2))
                    nc.gpsimd.tensor_tensor(veps[st][:, :], mv[st][:, :, 1], eps_sb[:, :], ALU.add).then_inc(veps_done[st], 1)
                    pool.wait_ge(veps_done[st], at(turn, 2, n + 1))
                    nc.gpsimd.tensor_tensor(rstd[st][:, :], veps[st][:, :], minus_half[:, :], ALU.pow).then_inc(rstd_done[st], 1)
                if stage == "weight" and layer == 0:
                    pool.wait_ge(exp_ok[st], at(turn, UNITS, k + 1))
                    pool.sem_inc(cut_begun[st], 1)
                    p = probs[st][:, k % NPROB, :, :]
                    nc.gpsimd.affine_select(out=p, in_=p, compare_op=ALU.is_ge, fill=0.0, base=0,
                                            pattern=[[0, NG], [1, 128]],
                                            channel_multiplier=-1).then_inc(cut_ok[st], 1)

            turns(pool, step)

        @block.scalar
        def _(act):
            act.wait_ge(c_in, 16)
            act.wait_ge(ones_ok, 1)
            nc.scalar.activation(sc_sb[0:HALF, :, :], c_sb[0:HALF, :, :], ACT.Silu).then_inc(silu_ok, 1)
            act.wait_ge(ident_ok, 2)
            nc.scalar.copy(ident16[:, :], ident[:, :]).then_inc(consts_ok, 1)
            nc.scalar.copy(identb[:, :], ident[:, :]).then_inc(consts_ok, 1)
            act.wait_ge(const_in, 32)
            def first(name, k):
                if name == "ada":
                    act.wait_ge(ada_ps[k], 1)
                    nc.scalar.copy(mod_f[k][:, :].rearrange("p (a n) -> p a n", a=2),
                                   ps[k][0:MREP, 0:2, 0:MOD // 2]).then_inc(ada_sb[k], 1)
                else:
                    l, part, c = k // 8, k // 4 % 2, k % 4
                    cols = slice(0, 3 * D) if part == 0 else slice(3 * D, RAWCOLS)
                    act.wait_ge(wraw_in[l][part], 16)
                    wait(act, w_ok, k - 1)
                    nc.scalar.activation(w_t[:, k % 2, 0:cols.stop - cols.start], w_raw[l][:, c, cols], ACT.Copy,
                                         scale=wmask_sb[:, c:c + 1]).then_inc(w_lo, 1)

            for k in range(4):
                first("weights", k)
            first("ada", 0)

            def step(stage, k, layer, st, it, turn):
                if stage == "turn_h":
                    n = k
                    bank = 2 if n == 0 else 0
                    act.wait_ge(hT_ps[st], at(turn, 2, n + 1))
                    if n == 0:
                        wait(act, f_ps[st], at(turn, 3, 0))
                    else:
                        act.wait_ge(qk_ps[st], at(turn, 4, 4))
                        act.wait_ge(v_ps[st], at(turn, 1, 1))
                    nc.scalar.copy(hT[st][:, :, :],
                                   ps[st][0:KR, bank, :].bitcast(F16).rearrange("p (c t) -> p c t", c=CH)
                                   ).then_inc(hT_sb[st], 1)
                if stage == "v":
                    act.wait_ge(v_ps[st], at(turn, 1, 1))
                    wait(act, av_ps[st], at(turn, UNITS, 0))
                    nc.scalar.activation(v_aug[st][:, :, :, 0:HD],
                                         ps[st][:, 3, 0:2 * D].rearrange("p (b h d) -> p b h d", b=2, h=H),
                                         ACT.Copy, scale=1.0 / WS).then_inc(v_sb[st], 1)
                if stage == "qk":
                    act.wait_ge(qk_ps[st], at(turn, 4, k + 1))
                    wait(act, qk_ok[st], at(turn, 4, 0))
                    nc.scalar.activation(qk_lo[st][:, k, :], ps[st][:, k, :], ACT.Copy,
                                         scale=qkmask_sb[:, k // 2:k // 2 + 1]).then_inc(qk_hi[st], 1)
                if stage == "maxima":
                    b = k
                    act.wait_ge(mT_ps[st], at(turn, 2, b + 1))
                    wait(act, m_moved[st][b], at(turn, 16, 0))
                    nc.scalar.copy(mrow[st][b][:, :, :],
                                   ps[st][0:NJ, 3 - b, 0:256].bitcast(F16).rearrange("p (g q) -> p g q", g=NG)
                                   ).then_inc(mT_sb[st], 1)
                if stage == "weight":
                    act.wait_ge(st_ps[st], at(turn, UNITS, k + 1))
                    wait(act, av_ps[st], at(turn, UNITS, k + 1 - NPROB))
                    nc.scalar.activation(probs[st][:, k % NPROB, :, :],
                                         ps[st][:, k % 2, :].rearrange("p (g q) -> p g q", g=NG),
                                         ACT.Exp, scale=float(HD) ** -0.5).then_inc(exp_ok[st], 1)
                if stage == "values_out":
                    b = k
                    act.wait_ge(av_ps[st], at(turn, UNITS, NJ * (b + 1)))
                    wait(act, on_ps[st], at(turn, 2, b))
                    nc.scalar.copy(oT[st][:, :, :],
                                   ps[st][:, 2, :].rearrange("p (g q) -> p g q", g=NG)).then_inc(o_sb[st], 1)
                if stage == "by_channel":
                    b = k
                    act.wait_ge(onT_ps[st], at(turn, 2, b + 1))
                    wait(act, pj_ps[st], at(turn, 1, 0))
                    nc.scalar.copy(onT[st][:, b, :, :],
                                   ps[st][0:HALF + 1, 3 - b, 0:256].rearrange("p (c q) -> p c q", c=2)
                                   ).then_inc(onT_sb[st], 1)
                if stage == "hidden":
                    func = ACT.Silu if layer == 0 else ACT.Gelu_apprx_tanh
                    act.wait_ge(f_ps[st], at(turn, 3, k + 1))
                    wait(act, y_ps[st], at(turn, 1, 0))
                    if k < 2:
                        o = ffT[st][:, 2 * k:2 * k + 2, :]
                        i = ps[st][:, 1 + k, :].rearrange("p (c t) -> p c t", c=2)
                    else:
                        o = ffT[st][0:FLAST, FCH - 1, :]
                        i = ps[st][0:FLAST, 3, 0:TOK]
                    nc.scalar.activation(o, i, func, scale=1.0 / WS).then_inc(f_sb[st], 1)

            turns(act, step, first)

        @block.vector
        def _(dve):
            nc.vector.memset(sc_sb[:, :, :], 1.0).then_inc(ones_ok, 1)
            for l in range(2):
                nc.vector.memset(h_cat[l][:, :, 3 * D:CAT], 1.0).then_inc(ones_ok, 1)
                nc.vector.memset(v_aug[l][:, :, :, HD], 1.0).then_inc(ones_ok, 1)
                nc.vector.memset(o_nat[l][:, :, :, HALF], 1.0).then_inc(ones_ok, 1)
                nc.vector.memset(ffT[l][64:128, FCH - 1, :], 1.0).then_inc(ones_ok, 1)
            dve.wait_ge(sel_in, 16)
            nc.vector.tensor_copy(sel[:, :, :], selc[:, :].unsqueeze(2).broadcast_to([MREP, B, 128])).then_inc(sel_ok, 1)
            dve.wait_ge(const_in, 32)

            def first(name, k):
                if name == "ada":
                    f, p = mod_f[k], mod_b[k]
                    dve.wait_ge(ada_sb[k], 1)
                    scales = f[:, :].rearrange("p (a s n) -> p a s n", a=2, s=3)[:, :, 1, :]
                    nc.vector.tensor_scalar(scales, scales, 1.0, None, ALU.add).then_inc(ada_one[k], 1)
                    dve.wait_ge(ada_one[k], 1)
                    nc.vector.tensor_copy(p[:, :], f[:, :]).then_inc(ada_split[k], 1)
                    dve.wait_ge(ada_split[k], 1)
                    nc.vector.tensor_tensor(p[32:64, :], f[32:64, :], p[32:64, :], ALU.subtract).then_inc(mod_ok[k], 1)
                else:
                    l, part, c = k // 8, k // 4 % 2, k % 4
                    dve.wait_ge(w_lo, k + 1)
                    t, raw = w_t[:, k % 2, :], w_raw[l][:, c, :]

                    def parts(out, cols, of=lambda a: a):
                        return nc.vector.scalar_tensor_tensor(
                            out=out, in0=of(raw[:, cols]), scalar=WS,
                            in1=of(t[:, cols] if part == 0 else t[:, 0:FF]), op0=ALU.mult, op1=ALU.subtract)

                    if part == 0:
                        slots = w16[l][:, c, 0:QK].rearrange("p (h s) -> p h s", s=SLOT)
                        for r in range(3):
                            parts(slots[:, :, r * HD:(r + 1) * HD], slice(0, 2 * D),
                                  lambda a: a.rearrange("p (h d) -> p h d", d=HD))
                        parts(w16[l][:, c, QK:QK + D], slice(2 * D, 3 * D)).then_inc(w_ok, 1)
                    else:
                        parts(w16[l][:, c, QK + D:WCOLS], slice(3 * D, RAWCOLS)).then_inc(w_ok, 1)

            for k in range(4):
                first("weights", k)
            first("ada", 0)

            def norm_stats(st, turn, n, x_sb, mod_at):
                for b in range(2):
                    nc.vector.bn_stats(out=stats[st][:, b, :], in_=x_sb[:, b, :]).then_inc(st_done[st], 1)
                dve.wait_ge(st_done[st], at(turn, 4, 2 * n + 2))
                dve.sem_inc(aggr_begun[st], 1)
                for b in range(2):
                    nc.vector.bn_aggr(out=mv[st][:, b, :], in_=stats[st][:, b, :]).then_inc(mv_done[st], 1)
                dve.wait_ge(mv_done[st], at(turn, 4, 2 * n + 2))
                dve.wait_ge(mod_ps[st], at(turn, 2, n + 1))
                for b in range(2):
                    nc.vector.scalar_tensor_tensor(out=ln_t[st][:, b, :], in0=x_sb[:, b, :], scalar=mv[st][:, b, 0:1],
                                                   in1=mod_at(b)[:, D:2 * D], op0=ALU.subtract,
                                                   op1=ALU.mult).then_inc(t_done[st], 1)

            def norm_rows(st, turn, n, mod_at):
                dve.wait_ge(rstd_done[st], at(turn, 2, n + 1))
                for b in range(2):
                    dve.wait_ge(t_done[st], at(turn, 4, 2 * n + b + 1))
                    nc.vector.scalar_tensor_tensor(out=ln_h[st][:, b, :], in0=ln_t[st][:, b, :],
                                                   scalar=rstd[st][:, b:b + 1], in1=mod_at(b)[:, 0:D],
                                                   op0=ALU.mult, op1=ALU.add).then_inc(h_done[st], 1)

            def norm_parts(st, turn, n):
                dve.wait_ge(h_done[st], at(turn, 4, 2 * n + 2))
                wait(dve, hT_ps[st], at(turn, 2, n))
                for p in range(2):
                    nc.vector.tensor_copy(h_cat[st][:, :, p * D:(p + 1) * D], ln_h[st][:, :, :]).then_inc(hi_done[st], 1)
                dve.wait_ge(hi_done[st], at(turn, 4, 2 * n + 1))
                nc.vector.tensor_tensor(h_cat[st][:, :, 2 * D:3 * D], ln_h[st][:, :, :], h_cat[st][:, :, 0:D],
                                        ALU.subtract).then_inc(hcat_ok[st], 1)

            def residual(st, turn, n, x_sb, x_out, done):
                nc.vector.tensor_copy(gated[st][:, :, :],
                                      ps[st][:, 1, 0:2 * D].rearrange("p (b d) -> p b d", b=2)).then_inc(gated_ok[st], 1)
                dve.wait_ge(gated_ok[st], at(turn, 4, 2 * n + 1))
                nc.vector.tensor_tensor(gated[st][:, :, :], ps[st][:, 0, 0:2 * D].rearrange("p (b d) -> p b d", b=2),
                                        gated[st][:, :, :], ALU.mult).then_inc(gated_ok[st], 1)
                dve.wait_ge(gated_ok[st], at(turn, 4, 2 * n + 2))
                nc.vector.tensor_tensor(x_out[:, :, :], x_sb[:, :, :], gated[st][:, :, :], ALU.add).then_inc(done, 1)

            def step(stage, k, layer, st, it, turn):
                b0 = first_row(st, it)
                x_lay = x_next[st] if layer == 1 else x_all[:, bass.ds(b0, 2), :]
                x_sb = x_mid[st] if k == 1 else x_lay
                first = 2 * k
                if stage == "norm_stats":
                    if k == 1:
                        dve.wait_ge(xmid_ok[st], at(turn, 1, 1))
                    elif layer == 0:
                        early = st == 0 and isinstance(it, int) and it == 0
                        dve.wait_ge(x_in[0 if early else 1], 16)
                    else:
                        dve.wait_ge(xout_ok[st], at(turn, 1, 0))
                    norm_stats(st, turn, k, x_sb, lambda b: ps[st][:, first + b, :])
                if stage == "norm_rows":
                    norm_rows(st, turn, k, lambda b: ps[st][:, first + b, :])
                if stage == "norm_parts":
                    norm_parts(st, turn, k)
                if stage == "qk":
                    dve.wait_ge(qk_hi[st], at(turn, 4, k + 1))
                    wait(dve, st_ps[st], at(turn, UNITS, 0))
                    nc.vector.scalar_tensor_tensor(
                        out=qkT[st][:, 2 * k:2 * k + 2, :].rearrange("p g t -> p (g t)"),
                        in0=ps[st][:, k, :], scalar=1.0 / WS, in1=qk_lo[st][:, k, :],
                        op0=ALU.mult, op1=ALU.subtract).then_inc(qk_ok[st], 1)
                if stage == "score":
                    b, j = k // NJ, k % NJ
                    dve.wait_ge(s_ps[st], at(turn, UNITS, k + 1))
                    nc.vector.tensor_reduce(mx[st][:, b, j, :], ps[st][:, k % 4, :].rearrange("p (g k) -> p g k", g=NG),
                                            AX_X, ALU.max).then_inc(mx_ok[st], 1)
                    if j == NJ - 1:
                        dve.wait_ge(mx_ok[st], at(turn, UNITS, k + 1))
                        wait(dve, mT_ps[st], at(turn, 2, 0))
                        nc.vector.tensor_scalar(mneg[st][:, b, :, :], mx[st][:, b, :, :].rearrange("p j g -> p g j"),
                                                -1.0 / MS, None, ALU.mult).then_inc(mneg_ok[st], 1)
                if stage == "by_query":
                    b = k
                    dve.wait_ge(on_ps[st], at(turn, 2, b + 1))
                    heads = ps[st][:, 3 - b, :].rearrange("p (h s) -> p h s", h=H)
                    nc.vector.reciprocal(out=rden[st][:, b, :], in_=heads[:, :, HD]).then_inc(rden_ok[st], 1)
                    dve.wait_ge(rden_ok[st], at(turn, 2, b + 1))
                    wait(dve, onT_ps[st], at(turn, 2, 0))
                    for c in range(2):
                        hs = slice(c * H // 2, (c + 1) * H // 2)
                        nc.vector.tensor_tensor(
                            o_nat[st][:, b, c, 0:HALF].rearrange("p (h d) -> p h d", d=HD), heads[:, hs, 0:HD],
                            rden[st][:, b, hs].unsqueeze(2).broadcast_to([128, H // 2, HD]),
                            ALU.mult).then_inc(on_ok[st], 1)
                if stage == "project":
                    dve.wait_ge(pj_ps[st], at(turn, 1, 1))
                    residual(st, turn, 0, x_lay, x_mid[st], xmid_ok[st])
                if stage == "mlp_out":
                    dve.wait_ge(y_ps[st], at(turn, 1, 1))
                    if layer == 0:
                        residual(st, turn, 1, x_mid[st], x_next[st], xout_ok[st])
                    else:
                        dve.wait_ge(y_stored[st], at(it, 16, 16))
                        residual(st, turn, 1, x_mid[st], x_fin[st], xout_ok[st])

            turns(dve, step, first)

        @block.tensor
        def _(pe):
            def first(name, k):
                if name == "ada":
                    pe.wait_ge(silu_ok, 1)
                    pe.wait_ge(wa_in[k], 16)
                    for n in range(2):
                        for c in range(2):
                            last = nc.tensor.matmul(ps[k][0:MREP, n, 0:MOD // 2], sc_sb[:, c, :],
                                                    wa_sb[k][:, c, n * MOD // 2:(n + 1) * MOD // 2],
                                                    start=(c == 0), stop=(c == 1))
                    last.then_inc(ada_ps[k], 1)

            first("ada", 0)
            pe.wait_ge(sel_ok, 1)
            pe.wait_ge(consts_ok, 2)
            pe.wait_ge(ones_ok, 9)

            def modulation(layer, st, it, at_b, cols):
                for b in range(2):
                    n = cols.stop - cols.start
                    last = nc.tensor.matmul(at_b(b), sel[:, bass.ds(first_row(st, it) + b, 1), :].rearrange("p a t -> p (a t)"),
                                            mod_b[layer][:, cols], start=True, stop=True)
                return last

            def transpose_h(st, bank):
                dst = ps[st][0:KR, bank, :].bitcast(F16).rearrange("p (c t) -> p c t", c=CH)
                for b in range(2):
                    for c in range(CH):
                        last = nc.tensor.transpose(dst[:, c, b * T:(b + 1) * T],
                                                   h_cat[st][:, b, c * KR:(c + 1) * KR], ident16[:, :])
                return last

            def stacked(out, layer, st, cols):
                for c in range(CH):
                    last = nc.tensor.matmul(out, w16[layer][:, c, cols], hT[st][:, c, :], start=(c == 0), stop=(c == CH - 1))
                return last

            def q_and_k(layer, st, gp):
                for n in range(2):
                    g = 2 * gp + n
                    last = stacked(ps[st][:, gp, n * TOK:(n + 1) * TOK], layer, st, slice(g * 128, (g + 1) * 128))
                last.then_inc(qk_ps[st], 1)

            def scores(layer, st, u):
                b, r = u // NJ, SLOT * (u % NJ)
                ts = slice(b * T, (b + 1) * T)
                if layer == 0:
                    nc.tensor.matmul(ps[st][:, u % 4, :], identb[:, :], causal[:, :, :], start=True, stop=False,
                                     skip_group_check=True)
                for g in range(NG):
                    last = nc.tensor.matmul(ps[st][:, u % 4, g * 128:(g + 1) * 128], qkT[st][r:r + PARTS, g, ts],
                                            qkT[st][r:r + PARTS, NG + g, ts], start=(layer == 1), stop=True,
                                            skip_group_check=True)
                last.then_inc(s_ps[st], 1)

            def scores_by_key(st, u):
                b, r = u // NJ, SLOT * (u % NJ)
                ts = slice(b * T, (b + 1) * T)
                for g in range(NG):
                    last = nc.tensor.matmul(ps[st][:, u % 2, g * 128:(g + 1) * 128],
                                            qkT[st][r:r + MROW + 1, NG + g, ts], qkT[st][r:r + MROW + 1, g, ts],
                                            start=True, stop=True, skip_group_check=True)
                last.then_inc(st_ps[st], 1)

            def values(st, u):
                b, j = u // NJ, u % NJ
                for g in range(NG):
                    last = nc.tensor.matmul(ps[st][SLOT * j:SLOT * j + HD + 1, 2, g * 128:(g + 1) * 128],
                                            v_aug[st][:, b, NJ * g + j, :], probs[st][:, u % NPROB, g, :],
                                            start=True, stop=True, skip_group_check=True)
                last.then_inc(av_ps[st], 1)

            def maxima(st, b):
                dst = ps[st][0:NJ, 3 - b, 0:256].bitcast(F16).rearrange("p (g q) -> p g q", g=NG)
                for g in range(NG):
                    last = nc.tensor.transpose(dst[:, g, :], mneg[st][:, b, g, :], ident16[:, :])
                last.then_inc(mT_ps[st], 1)

            def by_query(st, b):
                for g in range(NG):
                    last = nc.tensor.transpose(ps[st][:, 3 - b, g * 128:(g + 1) * 128], oT[st][:, g, :], ident[:, :])
                last.then_inc(on_ps[st], 1)

            def by_channel(st, b):
                for c in range(2):
                    last = nc.tensor.transpose(ps[st][0:HALF + 1, 3 - b, c * 128:(c + 1) * 128],
                                               o_nat[st][:, b, c, :], ident[:, :])
                last.then_inc(onT_ps[st], 1)

            def step(stage, k, layer, st, it, turn):
                if stage == "norm_stats" and k == 0:
                    pe.wait_ge(mod_ok[layer], 1)
                    wait(pe, xout_ok[st], at(turn, 1, 0))
                    modulation(layer, st, it, lambda b: ps[st][:, b, 0:2 * D], slice(0, 2 * D)).then_inc(mod_ps[st], 1)
                if stage == "turn_h":
                    pe.wait_ge(hcat_ok[st], at(turn, 2, k + 1))
                    transpose_h(st, 2 if k == 0 else 0).then_inc(hT_ps[st], 1)
                if stage == "v":
                    pe.wait_ge(hT_sb[st], at(turn, 2, 1))
                    pe.wait_ge(kconst_in, 32)
                    pe.wait_ge(w_ok, 8 * layer + 4)
                    for b in range(2):
                        for c in range(CH):
                            last = nc.tensor.matmul(ps[st][:, 3, b * D:(b + 1) * D], hT[st][:, c, b * T:(b + 1) * T],
                                                    w16[layer][:, c, QK:QK + D], start=(c == 0), stop=(c == CH - 1))
                    last.then_inc(v_ps[st], 1)
                if stage == "qk":
                    if k == 3:
                        pe.wait_ge(v_sb[st], at(turn, 1, 1))
                    q_and_k(layer, st, k)
                if stage == "score":
                    if k == 0:
                        pe.wait_ge(qk_ok[st], at(turn, 4, 4))
                    if k >= 4:
                        pe.wait_ge(mx_ok[st], at(turn, UNITS, k - 3))
                    if k == 7:
                        pe.wait_ge(mT_sb[st], at(turn, 2, 1))
                    scores(layer, st, k)
                if stage == "maxima":
                    pe.wait_ge(mneg_ok[st], at(turn, 2, k + 1))
                    maxima(st, k)
                if stage == "weight":
                    if k == 0:
                        pe.wait_ge(mx_ok[st], at(turn, UNITS, 6))
                    if k >= 2:
                        pe.wait_ge(exp_ok[st], at(turn, UNITS, k - 1))
                    pe.wait_ge(m_moved[st][k // NJ], at(turn, 16, 16))
                    scores_by_key(st, k)
                if stage == "value":
                    if layer == 0:
                        pe.wait_ge(cut_ok[st], at(it, UNITS, k + 1))
                    else:
                        pe.wait_ge(exp_ok[st], at(turn, UNITS, k + 1))
                    if k == 0:
                        pe.wait_ge(mT_sb[st], at(turn, 2, 2))
                    if k == NJ:
                        pe.wait_ge(o_sb[st], at(turn, 2, 1))
                    values(st, k)
                if stage == "by_query":
                    pe.wait_ge(o_sb[st], at(turn, 2, k + 1))
                    by_query(st, k)
                if stage == "by_channel":
                    pe.wait_ge(on_ok[st], at(turn, 4, 2 * k + 2))
                    by_channel(st, k)
                if stage == "project":
                    pe.wait_ge(exp_ok[st], at(turn, UNITS, UNITS))
                    modulation(layer, st, it, lambda b: ps[st][:, 1, b * D:(b + 1) * D], slice(2 * D, 3 * D))
                    pe.wait_ge(onT_sb[st], at(turn, 2, 2))
                    pe.wait_ge(wp_in[layer], 32)
                    for b in range(2):
                        for c in range(2):
                            rows = HALF + 1 - c
                            last = nc.tensor.matmul(ps[st][:, 0, b * D:(b + 1) * D], onT[st][0:rows, b, c, :],
                                                    wp_sb[layer][0:rows, c, :], start=(c == 0), stop=(c == 1))
                    last.then_inc(pj_ps[st], 1)
                    modulation(layer, st, it, lambda b: ps[st][:, 2 + b, 0:2 * D],
                               slice(3 * D, 5 * D)).then_inc(mod_ps[st], 1)
                if stage == "hidden":
                    if k == 0:
                        pe.wait_ge(hT_sb[st], at(turn, 2, 2))
                        pe.wait_ge(w_ok, 8 * layer + 8)
                    for m in range(2 * k, min(2 * k + 2, FCH)):
                        rows = 128 if m < FCH - 1 else FLAST
                        w0 = QK + D + 128 * m
                        last = stacked(ps[st][0:rows, 1 + k, (m % 2) * TOK:(m % 2 + 1) * TOK], layer, st,
                                       slice(w0, w0 + rows))
                    last.then_inc(f_ps[st], 1)
                if stage == "mlp_out":
                    pe.wait_ge(f_sb[st], at(turn, 3, 1))
                    modulation(layer, st, it, lambda b: ps[st][:, 1, b * D:(b + 1) * D], slice(5 * D, 6 * D))
                    pe.wait_ge(f_sb[st], at(turn, 3, 3))
                    for b in range(2):
                        for m in range(FCH):
                            rows = 128 if m < FCH - 1 else FLAST + 1
                            last = nc.tensor.matmul(ps[st][:, 0, b * D:(b + 1) * D], ffT[st][0:rows, m, b * T:(b + 1) * T],
                                                    w2_sb[layer][0:rows, m, :], start=(m == 0), stop=(m == FCH - 1))
                    last.then_inc(y_ps[st], 1)

            turns(pe, step, first)


def _layout(inputs):
    import numpy as np

    f = {k: np.asarray(v) for k, v in inputs.items()}

    def cat(w, bias):
        rows = np.concatenate([w, w, w, bias[None], bias[None], np.zeros((CAT - 3 * D - 2, RAWCOLS), w.dtype)], axis=0)
        return np.ascontiguousarray(rows.reshape(CH, KR, RAWCOLS).transpose(1, 0, 2))

    def halves(w, bias):
        o = np.zeros((HALF + 1, 2, w.shape[1]), w.dtype)
        o[:HALF] = w.reshape(2, HALF, -1).transpose(1, 0, 2)
        o[HALF, 0] = bias
        return o

    def hidden(w, bias):
        o = np.zeros((FCH * 128, w.shape[1]), w.dtype)
        o[:FF] = w
        o[FF] = bias
        return np.ascontiguousarray(o.reshape(FCH, 128, -1).transpose(1, 0, 2))

    a = {"x": f["x"]}
    w = np.concatenate([f["L0_cond_Wq"], f["L0_cond_Wk"], f["L0_cond_Wv"], f["L0_cond_W1"]], axis=1)
    a["w_cat0"] = cat(w, np.concatenate([np.zeros(3 * D, w.dtype), f["L0_cond_b1"]]))
    a["w_cat1"] = cat(np.concatenate([f["L1_cond_W_qkv"], f["L1_cond_W_fc1"]], axis=1),
                      np.concatenate([f["L1_cond_b_qkv"], f["L1_cond_b_fc1"]]))
    a["w_proj0"] = halves(f["L0_cond_Wp"], f["L0_cond_bp"])
    a["w_proj1"] = halves(f["L1_cond_W_proj"], f["L1_cond_b_proj"])
    a["w_fc2_0"] = hidden(f["L0_cond_W2"], f["L0_cond_b2"])
    a["w_fc2_1"] = hidden(f["L1_cond_W_fc2"], f["L1_cond_b_fc2"])
    a["w_ada0"] = halves(f["L0_cond_Wa"], f["L0_cond_ba"])
    a["w_ada1"] = halves(f["L1_cond_W_ada"], f["L1_cond_b_ada"])
    c = f["cond_1152"]
    c_rep = np.zeros((HALF + 1, 2, MREP), c.dtype)
    for p in range(2):
        c_rep[:HALF, :, 32 * p:32 * p + B] = c.T.reshape(2, HALF, B).transpose(1, 0, 2)
    a["c_rep"] = c_rep
    r = np.arange(CAT).reshape(CH, KR).T
    low = ((r >= D) & (r < 2 * D)) | (r == 3 * D + 1)
    a["wmask"] = np.ascontiguousarray(np.where(low, WS, 0.0).astype(np.float32))
    slot = np.arange(128) % SLOT
    q_low = (slot >= 2 * HD) & (slot < 3 * HD)
    k_low = (slot >= HD) & (slot < 2 * HD)
    a["qkmask"] = np.stack([np.where(q_low, 1 / WS, 0.0), np.where(k_low, 1 / WS, 0.0)], axis=1).astype(np.float32)
    a["batch_sel"] = ((np.arange(MREP)[:, None] % 32 == np.arange(B)[None])
                      & (np.arange(MREP)[:, None] < 64)).astype(np.float32)
    a["k_const"] = np.full((1, H, 1), MS * WS, np.float16)
    return a


def kernel(**inputs):
    import concourse.bacc as bacc
    import numpy as np
    from concourse.bass_utils import run_bass_kernel_spmd

    nc = bacc.Bacc("TRN2", target_bir_lowering=False, num_devices=1)
    arrays = _layout(inputs)
    ap = {n: nc.dram_tensor(n + "_dram", a.shape, mybir.dt.from_np(a.dtype), kind="ExternalInput").ap()
          for n, a in arrays.items()}
    out = nc.dram_tensor("out_dram", (B, T, D), F32, kind="ExternalOutput").ap()
    two_layer_kernel(nc, ap["x"], ap["c_rep"], [ap["w_cat0"], ap["w_cat1"]], [ap["w_proj0"], ap["w_proj1"]],
                     [ap["w_fc2_0"], ap["w_fc2_1"]], [ap["w_ada0"], ap["w_ada1"]], ap["wmask"], ap["qkmask"],
                     ap["batch_sel"], ap["k_const"], out)
    r = run_bass_kernel_spmd(nc, [{n + "_dram": a for n, a in arrays.items()}], core_ids=[0])
    return np.asarray(r.results[0]["out_dram"])
```

```python
from contextlib import ExitStack

import concourse.bass as bass
from concourse import mybir

F32 = mybir.dt.float32
F16 = mybir.dt.float16
BF16 = mybir.dt.bfloat16
ALU = mybir.AluOpType
ACT = mybir.ActivationFunctionType
AX_X = mybir.AxisListType.X

B, T, D = 16, 128, 144
H = 16
HD = D // H
FF = 4 * D
EPS = 1e-6
PAIRS = B // 4
TOK = 2 * T

NJ, NG = 4, 4
SLOT = 128 // NJ
PARTS = 3 * HD
MROW = PARTS + 1
MS = 64.0

UNITS = 2 * NJ
NPROB = 4

CH = 4
KR = 109
CAT = CH * KR
QK = 2 * NG * 128
WCOLS = QK + D + FF
RAWCOLS = 3 * D + FF
BIAS_ROW = (3 * D) % KR
WS = 16.0
HALF = D // 2
FCH = (FF + 127) // 128
FLAST = FF - 128 * (FCH - 1)
MOD = 6 * D
MREP = 96


WAYS = [[("norm_stats", 0, -3.6), ("norm_rows", 0, -3.5), ("norm_parts", 0, 0.2), ("turn_h", 0, 0.9),
         ("v", 0, 3.4), ("qk", 0, 3.6), ("qk", 1, 4.4), ("qk", 2, 5.5), ("qk", 3, 6.4), ("score", 0, 9.3),
         ("score", 1, 12.0), ("score", 2, 12.4), ("score", 3, 12.7), ("score", 4, 13.1), ("score", 5, 14.4),
         ("score", 6, 15.2), ("maxima", 0, 15.7), ("score", 7, 16.7), ("weight", 0, 18.6), ("maxima", 1, 19.0),
         ("weight", 1, 19.0), ("weight", 2, 20.2), ("weight", 3, 20.8), ("value", 0, 21.9), ("value", 1, 22.0),
         ("weight", 4, 22.5), ("weight", 5, 22.8), ("value", 2, 22.8), ("value", 3, 23.0),
         ("values_out", 0, 23.2), ("weight", 6, 23.2), ("weight", 7, 23.7), ("value", 4, 24.1),
         ("by_query", 0, 24.5), ("gate", 0, 24.5), ("value", 5, 24.9), ("value", 6, 25.4), ("value", 7, 25.8),
         ("values_out", 1, 25.9), ("by_channel", 0, 26.4), ("by_query", 1, 27.4), ("by_channel", 1, 29.8),
         ("project", 0, 30.6), ("norm_stats", 1, 32.1), ("norm_rows", 1, 35.3), ("norm_parts", 1, 36.5),
         ("turn_h", 1, 37.4), ("hidden", 0, 39.6), ("hidden", 1, 39.8), ("hidden", 2, 40.7), ("gate", 1, 41.9),
         ("mlp_out", 0, 43.5)],
        [("norm_stats", 0, -2.0), ("norm_rows", 0, -1.4), ("norm_parts", 0, 0.2), ("turn_h", 0, 1.8),
         ("v", 0, 2.9), ("qk", 0, 4.3), ("qk", 1, 5.9), ("qk", 2, 9.6), ("qk", 3, 10.8), ("score", 0, 11.9),
         ("score", 1, 12.7), ("score", 2, 13.1), ("score", 3, 13.2), ("score", 4, 14.4), ("score", 5, 14.5),
         ("score", 6, 15.3), ("maxima", 0, 15.6), ("score", 7, 17.1), ("weight", 0, 17.1), ("maxima", 1, 17.6),
         ("weight", 1, 18.1), ("weight", 2, 20.2), ("weight", 3, 20.4), ("value", 0, 21.0),
         ("weight", 4, 21.1), ("value", 1, 21.4), ("value", 2, 22.7), ("value", 3, 22.9),
         ("values_out", 0, 23.0), ("weight", 5, 23.4), ("weight", 6, 24.0), ("weight", 7, 24.2),
         ("by_query", 0, 24.2), ("value", 4, 24.5), ("value", 5, 25.4), ("value", 6, 25.5), ("value", 7, 25.8),
         ("values_out", 1, 26.3), ("by_query", 1, 27.6), ("by_channel", 0, 29.2), ("by_channel", 1, 29.5),
         ("gate", 0, 30.1), ("project", 0, 30.6), ("norm_stats", 1, 32.2), ("norm_rows", 1, 33.7),
         ("norm_parts", 1, 34.6), ("turn_h", 1, 37.3), ("hidden", 0, 39.7), ("hidden", 1, 40.2),
         ("hidden", 2, 40.6), ("gate", 1, 41.0), ("mlp_out", 0, 43.5)]]
SPAN = 47.8
FIRST = ([("weights", 4 + i, 12.0 + 2.5 * i) for i in range(4)] + [("ada", 1, 8.0)]
         + [("weights", 8 + i, 23.0 + 2.0 * i) for i in range(8)])
LAG = 23.8


def first_row(stream, pair):
    return 2 * (PAIRS * stream + pair)


def at(pair, per_pair, k):
    return pair * per_pair + k


def turned_bank(n, b):
    return b if n == 1 else 3 - b


def wait(eng, sem, value):
    if not (isinstance(value, int) and value <= 0):
        eng.wait_ge(sem, value)


def two_layer_kernel(nc, x, c_rep, w_cat, w_proj, w_fc2, w_ada, wmask, qkmask, batch_sel, k_const, out):
    ctx = ExitStack()
    with ctx:
        def sb(name, shape, dt):
            return ctx.enter_context(nc.sbuf_tensor(name, shape, dt))

        def sem(name):
            return ctx.enter_context(nc.semaphore(name))

        def both(make, name):
            return [make(f"{name}{l}") for l in range(2)]

        ident = sb("ident", [128, 128], F32)
        ident16 = sb("ident16", [128, 128], F16)
        identb = sb("identb", [128, 128], BF16)
        causal = sb("causal", [128, NG, 128], BF16)
        sel = sb("sel", [MREP, B, 128], F16)
        selc = sb("selc", [MREP, B], F32)
        wmask_sb = sb("wmask_sb", [KR, CH], F32)
        qkmask_sb = sb("qkmask_sb", [128, 2], F32)
        c_sb = sb("c_sb", [HALF + 1, 2, MREP], F32)
        sc_sb = sb("sc_sb", [HALF + 1, 2, MREP], F32)
        w_raw = [sb(f"w_raw{l}", [KR, CH, RAWCOLS], F32) for l in range(2)]
        w_t = sb("w_t", [KR, 2, FF], F16)
        x_all = sb("x_all", [128, B, D], F32)
        w16 = [sb(f"w16_{l}", [KR, CH, WCOLS], F16) for l in range(2)]
        wp_sb = [sb(f"wp_sb{l}", [HALF + 1, 2, D], F32) for l in range(2)]
        w2_sb = [sb(f"w2_sb{l}", [128, FCH, D], F32) for l in range(2)]
        wa_sb = [sb(f"wa_sb{l}", [HALF + 1, 2, MOD], F32) for l in range(2)]
        mod_f = [sb(f"mod_f{l}", [MREP, MOD], F32) for l in range(2)]
        mod_b = [sb(f"mod_b{l}", [MREP, MOD], F16) for l in range(2)]

        x_mid = [sb(f"x_mid{l}", [128, 2, D], F32) for l in range(2)]
        x_next = [sb(f"x_next{l}", [128, 2, D], F32) for l in range(2)]
        x_fin = [sb(f"x_fin{l}", [128, 2, D], F32) for l in range(2)]
        gate = [sb(f"gate{l}", [128, 2, D], F32) for l in range(2)]
        gated = [sb(f"gated{l}", [128, 2, D], F32) for l in range(2)]
        stats = [sb(f"stats{l}", [128, 2, 6], F32) for l in range(2)]
        mv = [sb(f"mv{l}", [128, 2, 2], F32) for l in range(2)]
        veps = [sb(f"veps{l}", [128, 2], F32) for l in range(2)]
        minus_half = sb("minus_half", [128, 2], F32)
        eps_sb = sb("eps_sb", [128, 2], F32)
        rstd = [sb(f"rstd{l}", [128, 2], F32) for l in range(2)]
        ln_t = [sb(f"ln_t{l}", [128, 2, D], F32) for l in range(2)]
        ln_h = [sb(f"ln_h{l}", [128, 2, D], F32) for l in range(2)]
        h_cat = [sb(f"h_cat{l}", [128, 2, CAT], F16) for l in range(2)]
        hT = [sb(f"hT{l}", [KR, CH, TOK], F16) for l in range(2)]
        v_aug = [sb(f"v_aug{l}", [128, 2, H, HD + 1], F32) for l in range(2)]
        qk_lo = [sb(f"qk_lo{l}", [128, 4, 2 * TOK], F16) for l in range(2)]
        qkT = [sb(f"qkT{l}", [128, 2 * NG, TOK], F16) for l in range(2)]
        mx = [sb(f"mx{l}", [128, 2, NJ, NG], F32) for l in range(2)]
        mneg = [sb(f"mneg{l}", [128, 2, NG, NJ], F16) for l in range(2)]
        mrow = [[sb(f"mrow{l}{b}", [NJ, NG, 128], F16) for b in range(2)] for l in range(2)]
        probs = [sb(f"probs{l}", [128, NPROB, NG, 128], F32) for l in range(2)]
        oT = [sb(f"oT{l}", [128, NG, 128], F32) for l in range(2)]
        rden = [sb(f"rden{l}", [128, 2, H], F32) for l in range(2)]
        o_nat = [sb(f"o_nat{l}", [128, 2, 2, HALF + 1], F32) for l in range(2)]
        onT = [sb(f"onT{l}", [HALF + 1, 2, 2, 128], F32) for l in range(2)]
        ffT = [sb(f"ffT{l}", [128, FCH, TOK], F32) for l in range(2)]
        ps = [ctx.enter_context(nc.psum_tensor(f"ps{l}", [128, 4, 512], F32)) for l in range(2)]

        const_in, sel_in, c_in = sem("const_in"), sem("sel_in"), sem("c_in")
        wraw_in = [[sem(f"wraw_in{l}{p}") for p in range(2)] for l in range(2)]
        kconst_in, spare_ok = sem("kconst_in"), sem("spare_ok")
        x_in = [sem(f"x_in{n}") for n in range(2)]
        wa_in, wp_in = both(sem, "wa_in"), both(sem, "wp_in")
        zeroed, ident_ok, consts_ok, ones_ok = sem("zeroed"), sem("ident_ok"), sem("consts_ok"), sem("ones_ok")
        sel_ok, silu_ok = sem("sel_ok"), sem("silu_ok")
        w_lo = sem("w_lo")
        w_ok = sem("w_ok")
        ada_ps, ada_sb = both(sem, "ada_ps"), both(sem, "ada_sb")
        ada_one, ada_split = both(sem, "ada_one"), both(sem, "ada_split")
        mod_ok = both(sem, "mod_ok")
        y_stored = both(sem, "y_stored")
        mod_ps = both(sem, "mod_ps")
        st_done = both(sem, "st_done")
        aggr_begun = both(sem, "aggr_begun")
        mv_done = both(sem, "mv_done")
        veps_done = both(sem, "veps_done")
        rstd_done = both(sem, "rstd_done")
        t_done = both(sem, "t_done")
        h_done = both(sem, "h_done")
        hi_done = both(sem, "hi_done")
        hcat_ok = both(sem, "hcat_ok")
        hi2_done = both(sem, "hi2_done")
        hT_ps = both(sem, "hT_ps")
        hT_sb = [[sem(f"hT_sb{l}{b}") for b in range(2)] for l in range(2)]
        v_ps, v_sb = both(sem, "v_ps"), both(sem, "v_sb")
        qk_ps = both(sem, "qk_ps")
        qk_hi = both(sem, "qk_hi")
        qk_ok = both(sem, "qk_ok")
        s_ps = both(sem, "s_ps")
        mx_ok = both(sem, "mx_ok")
        mneg_ok = both(sem, "mneg_ok")
        mT_ps, mT_sb = both(sem, "mT_ps"), both(sem, "mT_sb")
        m_moved = [[sem(f"m_moved{l}{b}") for b in range(2)] for l in range(2)]
        st_ps = both(sem, "st_ps")
        exp_ok = both(sem, "exp_ok")
        cut_begun = both(sem, "cut_begun")
        cut_ok = both(sem, "cut_ok")
        av_ps = both(sem, "av_ps")
        o_sb = both(sem, "o_sb")
        on_ps = both(sem, "on_ps")
        rden_ok = both(sem, "rden_ok")
        on_ok = both(sem, "on_ok")
        onT_ps, onT_sb = both(sem, "onT_ps"), both(sem, "onT_sb")
        gate_ps = both(sem, "gate_ps")
        gate_sb = both(sem, "gate_sb")
        pj_ps = both(sem, "pj_ps")
        gated_ok = both(sem, "gated_ok")
        xmid_ok = both(sem, "xmid_ok")
        f_ps, f_sb = both(sem, "f_ps"), both(sem, "f_sb")
        y_ps = both(sem, "y_ps")
        xout_ok = both(sem, "xout_ok")

        block = ctx.enter_context(nc.Block())

        lead = [(t + l * SPAN, 0, l, name, k) for l in range(2) for name, k, t in WAYS[l]]
        follow = [(t + LAG, 1, l, name, k) for t, _, l, name, k in lead]
        within = sorted(lead + [e for e in follow if e[0] < 2 * SPAN])
        over = sorted((t - 2 * SPAN, st, l, name, k) for t, st, l, name, k in follow if t >= 2 * SPAN)

        def turns(eng, step, first=lambda name, k: None):
            for _, st, l, name, k in sorted(within + [(t, 2, 0, name, k) for name, k, t in FIRST]):
                if st == 2:
                    first(name, k)
                else:
                    step(name, k, l, st, 0, l)
            with eng.Fori(1, PAIRS) as i:
                for t, st, l, name, k in sorted(within + [(t, 2, l, name, k) for t, _, l, name, k in over]):
                    if st == 2:
                        step(name, k, l, 1, i - 1, 2 * (i - 1) + l)
                    else:
                        step(name, k, l, st, i, 2 * i + l)
            for _, st, l, name, k in over:
                step(name, k, l, st, PAIRS - 1, 2 * (PAIRS - 1) + l)

        @block.sync
        def _(sp):
            for st in range(2):
                sp.sem_inc(y_stored[st], 16)
            sp.dma_start(c_sb[:, :, :], c_rep).then_inc(c_in, 16)
            sp.dma_start(wa_sb[0][:, :, :], w_ada[0]).then_inc(wa_in[0], 16)
            sp.dma_start(selc[:, :], batch_sel).then_inc(sel_in, 16)
            sp.dma_start(wmask_sb[:, :], wmask).then_inc(const_in, 16)
            sp.dma_start(qkmask_sb[:, :], qkmask).then_inc(const_in, 16)
            sp.dma_start(w_raw[0][:, :, 0:3 * D], w_cat[0][:, :, 0:3 * D]).then_inc(wraw_in[0][0], 16)
            sp.dma_start(x_all[:, 0:2, :], x[0:2, :, :].rearrange("b t d -> t b d")).then_inc(x_in[0], 16)
            sp.wait_ge(spare_ok, 2)
            for l in range(2):
                slots = w16[l][BIAS_ROW:BIAS_ROW + 1, CH - 1, QK // 2:QK].rearrange("p (h s) -> p h s", s=SLOT)
                sp.dma_start(slots[:, :, MROW:MROW + 1], k_const,
                             allow_slow_non_contiguous=True).then_inc(kconst_in, 16)
            sp.dma_start(w_raw[0][:, :, 3 * D:RAWCOLS], w_cat[0][:, :, 3 * D:RAWCOLS]).then_inc(wraw_in[0][1], 16)
            sp.dma_start(x_all[:, 2:B, :], x[2:B, :, :].rearrange("b t d -> t b d")).then_inc(x_in[1], 16)
            sp.dma_start(wa_sb[1][:, :, :], w_ada[1]).then_inc(wa_in[1], 16)
            sp.dma_start(wp_sb[0][:, :, :], w_proj[0]).then_inc(wp_in[0], 16)
            sp.dma_start(w2_sb[0][:, :, :], w_fc2[0]).then_inc(wp_in[0], 16)
            sp.dma_start(w_raw[1][:, :, 0:3 * D], w_cat[1][:, :, 0:3 * D]).then_inc(wraw_in[1][0], 16)
            sp.dma_start(w_raw[1][:, :, 3 * D:RAWCOLS], w_cat[1][:, :, 3 * D:RAWCOLS]).then_inc(wraw_in[1][1], 16)
            sp.dma_start(wp_sb[1][:, :, :], w_proj[1]).then_inc(wp_in[1], 16)
            sp.dma_start(w2_sb[1][:, :, :], w_fc2[1]).then_inc(wp_in[1], 16)

            def step(stage, k, layer, st, it, turn):
                if stage == "maxima":
                    b = k
                    sp.wait_ge(mT_sb[st], at(turn, 2, b + 1))
                    sp.dma_start(qkT[st][MROW:128:SLOT, 0:NG, b * T:(b + 1) * T],
                                 mrow[st][b][:, :, :]).then_inc(m_moved[st][b], 16)
                if stage == "mlp_out" and layer == 1:
                    sp.wait_ge(xout_ok[st], at(turn, 1, 1))
                    sp.dma_start(out[bass.ds(first_row(st, it), 2), :, :].rearrange("b t d -> t b d"),
                                 x_fin[st][:, :, :]).then_inc(y_stored[st], 16)

            turns(sp, step)
            for st in range(2):
                sp.wait_ge(y_stored[st], at(PAIRS, 16, 16))

        @block.gpsimd
        def _(pool):
            nc.gpsimd.memset(ident[:, :], 0.0).then_inc(zeroed, 1)
            nc.gpsimd.memset(causal[:, :, :], 0.0).then_inc(zeroed, 1)
            nc.gpsimd.memset(minus_half[:, :], -0.5).then_inc(zeroed, 1)
            nc.gpsimd.memset(eps_sb[:, :], EPS).then_inc(zeroed, 1)
            for l in range(2):
                spare = w16[l][:, :, 0:QK].rearrange("p c (h s) -> p c h s", s=SLOT)[:, :, :, PARTS:SLOT]
                nc.gpsimd.memset(spare, 0.0).then_inc(spare_ok, 1)
            pool.wait_ge(zeroed, 4)
            nc.gpsimd.affine_select(out=ident[:, :], in_=ident[:, :], compare_op=ALU.not_equal, fill=1.0,
                                    base=0, pattern=[[-1, 128]], channel_multiplier=1).then_inc(ident_ok, 1)
            nc.gpsimd.affine_select(out=causal[:, :, :], in_=causal[:, :, :], compare_op=ALU.is_ge, fill=-1e30,
                                    base=0, pattern=[[0, NG], [-1, 128]], channel_multiplier=1).then_inc(ident_ok, 1)

            def step(stage, k, layer, st, it, turn):
                if stage == "norm_stats":
                    n = k
                    pool.wait_ge(mv_done[st], at(turn, 4, 2 * n + 2))
                    nc.gpsimd.tensor_tensor(veps[st][:, :], mv[st][:, :, 1], eps_sb[:, :], ALU.add).then_inc(veps_done[st], 1)
                    pool.wait_ge(veps_done[st], at(turn, 2, n + 1))
                    nc.gpsimd.tensor_tensor(rstd[st][:, :], veps[st][:, :], minus_half[:, :], ALU.pow).then_inc(rstd_done[st], 1)
                if stage == "weight" and layer == 0:
                    pool.wait_ge(exp_ok[st], at(turn, UNITS, k + 1))
                    pool.sem_inc(cut_begun[st], 1)
                    p = probs[st][:, k % NPROB, :, :]
                    nc.gpsimd.affine_select(out=p, in_=p, compare_op=ALU.is_ge, fill=0.0, base=0,
                                            pattern=[[0, NG], [1, 128]],
                                            channel_multiplier=-1).then_inc(cut_ok[st], 1)

            turns(pool, step)

        @block.scalar
        def _(act):
            act.wait_ge(c_in, 16)
            act.wait_ge(ones_ok, 1)
            nc.scalar.activation(sc_sb[0:HALF, :, :], c_sb[0:HALF, :, :], ACT.Silu).then_inc(silu_ok, 1)
            act.wait_ge(ident_ok, 2)
            nc.scalar.copy(ident16[:, :], ident[:, :]).then_inc(consts_ok, 1)
            nc.scalar.copy(identb[:, :], ident[:, :]).then_inc(consts_ok, 1)
            act.wait_ge(const_in, 32)
            def first(name, k):
                if name == "ada":
                    act.wait_ge(ada_ps[k], 1)
                    nc.scalar.copy(mod_f[k][:, :].rearrange("p (a n) -> p a n", a=2),
                                   ps[k][0:MREP, 0:2, 0:MOD // 2]).then_inc(ada_sb[k], 1)
                else:
                    l, part, c = k // 8, k // 4 % 2, k % 4
                    cols = slice(0, 3 * D) if part == 0 else slice(3 * D, RAWCOLS)
                    act.wait_ge(wraw_in[l][part], 16)
                    wait(act, w_ok, k - 1)
                    nc.scalar.activation(w_t[:, k % 2, 0:cols.stop - cols.start], w_raw[l][:, c, cols], ACT.Copy,
                                         scale=wmask_sb[:, c:c + 1]).then_inc(w_lo, 1)

            for k in range(4):
                first("weights", k)
            first("ada", 0)

            def step(stage, k, layer, st, it, turn):
                if stage == "norm_parts":
                    act.wait_ge(h_done[st], at(turn, 4, 2 * k + 2))
                    wait(act, hT_ps[st], at(turn, 4, 2 * k))
                    nc.scalar.copy(h_cat[st][:, :, D:2 * D], ln_h[st][:, :, :]).then_inc(hi2_done[st], 1)
                if stage == "turn_h":
                    n = k
                    act.wait_ge(hT_ps[st], at(turn, 4, 2 * n + 1))
                    if n == 0:
                        wait(act, f_ps[st], at(turn, 3, 0))
                    else:
                        act.wait_ge(qk_ps[st], at(turn, 4, 4))
                        act.wait_ge(v_ps[st], at(turn, 1, 1))
                    src = ps[st][0:KR, turned_bank(n, 0), 0:TOK].bitcast(F16).rearrange("p (c t) -> p c t", c=CH)
                    nc.scalar.copy(hT[st][:, :, 0:T], src).then_inc(hT_sb[st][0], 1)
                if stage == "v":
                    act.wait_ge(v_ps[st], at(turn, 1, 1))
                    wait(act, av_ps[st], at(turn, UNITS, 0))
                    nc.scalar.activation(v_aug[st][:, :, :, 0:HD],
                                         ps[st][:, 3, 0:2 * D].rearrange("p (b h d) -> p b h d", b=2, h=H),
                                         ACT.Copy, scale=1.0 / WS).then_inc(v_sb[st], 1)
                if stage == "qk":
                    act.wait_ge(qk_ps[st], at(turn, 4, k + 1))
                    wait(act, qk_ok[st], at(turn, 4, 0))
                    nc.scalar.activation(qk_lo[st][:, k, :], ps[st][:, k, :], ACT.Copy,
                                         scale=qkmask_sb[:, k // 2:k // 2 + 1]).then_inc(qk_hi[st], 1)
                if stage == "maxima":
                    b = k
                    act.wait_ge(mT_ps[st], at(turn, 2, b + 1))
                    wait(act, m_moved[st][b], at(turn, 16, 0))
                    nc.scalar.copy(mrow[st][b][:, :, :],
                                   ps[st][0:NJ, 3 - b, 0:256].bitcast(F16).rearrange("p (g q) -> p g q", g=NG)
                                   ).then_inc(mT_sb[st], 1)
                if stage == "weight":
                    act.wait_ge(st_ps[st], at(turn, UNITS, k + 1))
                    wait(act, av_ps[st], at(turn, UNITS, k + 1 - NPROB))
                    nc.scalar.activation(probs[st][:, k % NPROB, :, :],
                                         ps[st][:, k % 2, :].rearrange("p (g q) -> p g q", g=NG),
                                         ACT.Exp, scale=float(HD) ** -0.5).then_inc(exp_ok[st], 1)
                if stage == "values_out":
                    b = k
                    act.wait_ge(av_ps[st], at(turn, UNITS, NJ * (b + 1)))
                    wait(act, on_ps[st], at(turn, 2, b))
                    nc.scalar.copy(oT[st][:, :, :],
                                   ps[st][:, 2, :].rearrange("p (g q) -> p g q", g=NG)).then_inc(o_sb[st], 1)
                if stage == "by_channel":
                    b = k
                    act.wait_ge(onT_ps[st], at(turn, 2, b + 1))
                    wait(act, pj_ps[st], at(turn, 1, 0))
                    nc.scalar.copy(onT[st][:, b, :, :],
                                   ps[st][0:HALF + 1, 3 - b, 0:256].rearrange("p (c q) -> p c q", c=2)
                                   ).then_inc(onT_sb[st], 1)
                if stage == "gate":
                    act.wait_ge(gate_ps[st], at(turn, 2, k + 1))
                    wait(act, gated_ok[st], at(turn, 2, k))
                    nc.scalar.copy(gate[st][:, :, :],
                                   ps[st][:, 1, 0:2 * D].rearrange("p (b d) -> p b d", b=2)).then_inc(gate_sb[st], 1)
                if stage == "hidden":
                    func = ACT.Silu if layer == 0 else ACT.Gelu_apprx_tanh
                    act.wait_ge(f_ps[st], at(turn, 3, k + 1))
                    wait(act, y_ps[st], at(turn, 1, 0))
                    if k < 2:
                        o = ffT[st][:, 2 * k:2 * k + 2, :]
                        i = ps[st][:, 1 + k, :].rearrange("p (c t) -> p c t", c=2)
                    else:
                        o = ffT[st][0:FLAST, FCH - 1, :]
                        i = ps[st][0:FLAST, 3, 0:TOK]
                    nc.scalar.activation(o, i, func, scale=1.0 / WS).then_inc(f_sb[st], 1)

            turns(act, step, first)

        @block.vector
        def _(dve):
            nc.vector.memset(sc_sb[:, :, :], 1.0).then_inc(ones_ok, 1)
            for l in range(2):
                nc.vector.memset(h_cat[l][:, :, 3 * D:CAT], 1.0).then_inc(ones_ok, 1)
                nc.vector.memset(v_aug[l][:, :, :, HD], 1.0).then_inc(ones_ok, 1)
                nc.vector.memset(o_nat[l][:, :, :, HALF], 1.0).then_inc(ones_ok, 1)
                nc.vector.memset(ffT[l][64:128, FCH - 1, :], 1.0).then_inc(ones_ok, 1)
            dve.wait_ge(sel_in, 16)
            nc.vector.tensor_copy(sel[:, :, :], selc[:, :].unsqueeze(2).broadcast_to([MREP, B, 128])).then_inc(sel_ok, 1)
            dve.wait_ge(const_in, 32)

            def first(name, k):
                if name == "ada":
                    f, p = mod_f[k], mod_b[k]
                    dve.wait_ge(ada_sb[k], 1)
                    scales = f[:, :].rearrange("p (a s n) -> p a s n", a=2, s=3)[:, :, 1, :]
                    nc.vector.tensor_scalar(scales, scales, 1.0, None, ALU.add).then_inc(ada_one[k], 1)
                    dve.wait_ge(ada_one[k], 1)
                    nc.vector.tensor_copy(p[:, :], f[:, :]).then_inc(ada_split[k], 1)
                    dve.wait_ge(ada_split[k], 1)
                    nc.vector.tensor_tensor(p[32:64, :], f[32:64, :], p[32:64, :], ALU.subtract).then_inc(mod_ok[k], 1)
                else:
                    l, part, c = k // 8, k // 4 % 2, k % 4
                    dve.wait_ge(w_lo, k + 1)
                    t, raw = w_t[:, k % 2, :], w_raw[l][:, c, :]

                    def parts(out, cols, of=lambda a: a):
                        return nc.vector.scalar_tensor_tensor(
                            out=out, in0=of(raw[:, cols]), scalar=WS,
                            in1=of(t[:, cols] if part == 0 else t[:, 0:FF]), op0=ALU.mult, op1=ALU.subtract)

                    if part == 0:
                        slots = w16[l][:, c, 0:QK].rearrange("p (h s) -> p h s", s=SLOT)
                        for r in range(3):
                            parts(slots[:, :, r * HD:(r + 1) * HD], slice(0, 2 * D),
                                  lambda a: a.rearrange("p (h d) -> p h d", d=HD))
                        parts(w16[l][:, c, QK:QK + D], slice(2 * D, 3 * D)).then_inc(w_ok, 1)
                    else:
                        parts(w16[l][:, c, QK + D:WCOLS], slice(3 * D, RAWCOLS)).then_inc(w_ok, 1)

            for k in range(4):
                first("weights", k)
            first("ada", 0)

            def norm_stats(st, turn, n, x_sb, mod_at):
                for b in range(2):
                    nc.vector.bn_stats(out=stats[st][:, b, :], in_=x_sb[:, b, :]).then_inc(st_done[st], 1)
                dve.wait_ge(st_done[st], at(turn, 4, 2 * n + 2))
                dve.sem_inc(aggr_begun[st], 1)
                for b in range(2):
                    nc.vector.bn_aggr(out=mv[st][:, b, :], in_=stats[st][:, b, :]).then_inc(mv_done[st], 1)
                dve.wait_ge(mv_done[st], at(turn, 4, 2 * n + 2))
                dve.wait_ge(mod_ps[st], at(turn, 2, n + 1))
                for b in range(2):
                    nc.vector.scalar_tensor_tensor(out=ln_t[st][:, b, :], in0=x_sb[:, b, :], scalar=mv[st][:, b, 0:1],
                                                   in1=mod_at(b)[:, D:2 * D], op0=ALU.subtract,
                                                   op1=ALU.mult).then_inc(t_done[st], 1)

            def norm_rows(st, turn, n, mod_at):
                dve.wait_ge(rstd_done[st], at(turn, 2, n + 1))
                wait(dve, hi2_done[st], at(turn, 2, n))
                for b in range(2):
                    dve.wait_ge(t_done[st], at(turn, 4, 2 * n + b + 1))
                    nc.vector.scalar_tensor_tensor(out=ln_h[st][:, b, :], in0=ln_t[st][:, b, :],
                                                   scalar=rstd[st][:, b:b + 1], in1=mod_at(b)[:, 0:D],
                                                   op0=ALU.mult, op1=ALU.add).then_inc(h_done[st], 1)

            def norm_parts(st, turn, n):
                dve.wait_ge(h_done[st], at(turn, 4, 2 * n + 2))
                wait(dve, hT_ps[st], at(turn, 4, 2 * n))
                nc.vector.tensor_copy(h_cat[st][:, :, 0:D], ln_h[st][:, :, :]).then_inc(hi_done[st], 1)
                dve.wait_ge(hi_done[st], at(turn, 2, n + 1))
                nc.vector.tensor_tensor(h_cat[st][:, :, 2 * D:3 * D], ln_h[st][:, :, :], h_cat[st][:, :, 0:D],
                                        ALU.subtract).then_inc(hcat_ok[st], 1)

            def residual(st, turn, n, x_sb, x_out, done):
                dve.wait_ge(gate_sb[st], at(turn, 2, n + 1))
                nc.vector.tensor_tensor(gated[st][:, :, :], ps[st][:, 0, 0:2 * D].rearrange("p (b d) -> p b d", b=2),
                                        gate[st][:, :, :], ALU.mult).then_inc(gated_ok[st], 1)
                dve.wait_ge(gated_ok[st], at(turn, 2, n + 1))
                nc.vector.tensor_tensor(x_out[:, :, :], x_sb[:, :, :], gated[st][:, :, :], ALU.add).then_inc(done, 1)

            def step(stage, k, layer, st, it, turn):
                b0 = first_row(st, it)
                x_lay = x_next[st] if layer == 1 else x_all[:, bass.ds(b0, 2), :]
                x_sb = x_mid[st] if k == 1 else x_lay
                first = 2 * k
                if stage == "norm_stats":
                    if k == 1:
                        dve.wait_ge(xmid_ok[st], at(turn, 1, 1))
                    elif layer == 0:
                        early = st == 0 and isinstance(it, int) and it == 0
                        dve.wait_ge(x_in[0 if early else 1], 16)
                    else:
                        dve.wait_ge(xout_ok[st], at(turn, 1, 0))
                    norm_stats(st, turn, k, x_sb, lambda b: ps[st][:, first + b, :])
                if stage == "norm_rows":
                    norm_rows(st, turn, k, lambda b: ps[st][:, first + b, :])
                if stage == "norm_parts":
                    norm_parts(st, turn, k)
                if stage == "turn_h":
                    n = k
                    dve.wait_ge(hT_ps[st], at(turn, 4, 2 * n + 2))
                    if n == 0:
                        wait(dve, f_ps[st], at(turn, 3, 0))
                    else:
                        dve.wait_ge(qk_ps[st], at(turn, 4, 4))
                        dve.wait_ge(v_ps[st], at(turn, 1, 1))
                    src = ps[st][0:KR, turned_bank(n, 1), 0:TOK].bitcast(F16).rearrange("p (c t) -> p c t", c=CH)
                    nc.vector.tensor_copy(hT[st][:, :, T:TOK], src).then_inc(hT_sb[st][1], 1)
                if stage == "qk":
                    dve.wait_ge(qk_hi[st], at(turn, 4, k + 1))
                    wait(dve, st_ps[st], at(turn, UNITS, 0))
                    nc.vector.scalar_tensor_tensor(
                        out=qkT[st][:, 2 * k:2 * k + 2, :].rearrange("p g t -> p (g t)"),
                        in0=ps[st][:, k, :], scalar=1.0 / WS, in1=qk_lo[st][:, k, :],
                        op0=ALU.mult, op1=ALU.subtract).then_inc(qk_ok[st], 1)
                if stage == "score":
                    b, j = k // NJ, k % NJ
                    dve.wait_ge(s_ps[st], at(turn, UNITS, k + 1))
                    nc.vector.tensor_reduce(mx[st][:, b, j, :], ps[st][:, k % 4, :].rearrange("p (g k) -> p g k", g=NG),
                                            AX_X, ALU.max).then_inc(mx_ok[st], 1)
                    if j == NJ - 1:
                        dve.wait_ge(mx_ok[st], at(turn, UNITS, k + 1))
                        wait(dve, mT_ps[st], at(turn, 2, 0))
                        nc.vector.tensor_scalar(mneg[st][:, b, :, :], mx[st][:, b, :, :].rearrange("p j g -> p g j"),
                                                -1.0 / MS, None, ALU.mult).then_inc(mneg_ok[st], 1)
                if stage == "by_query":
                    b = k
                    dve.wait_ge(on_ps[st], at(turn, 2, b + 1))
                    heads = ps[st][:, 3 - b, :].rearrange("p (h s) -> p h s", h=H)
                    nc.vector.reciprocal(out=rden[st][:, b, :], in_=heads[:, :, HD]).then_inc(rden_ok[st], 1)
                    dve.wait_ge(rden_ok[st], at(turn, 2, b + 1))
                    wait(dve, onT_ps[st], at(turn, 2, 0))
                    for c in range(2):
                        hs = slice(c * H // 2, (c + 1) * H // 2)
                        nc.vector.tensor_tensor(
                            o_nat[st][:, b, c, 0:HALF].rearrange("p (h d) -> p h d", d=HD), heads[:, hs, 0:HD],
                            rden[st][:, b, hs].unsqueeze(2).broadcast_to([128, H // 2, HD]),
                            ALU.mult).then_inc(on_ok[st], 1)
                if stage == "project":
                    dve.wait_ge(pj_ps[st], at(turn, 1, 1))
                    residual(st, turn, 0, x_lay, x_mid[st], xmid_ok[st])
                if stage == "mlp_out":
                    dve.wait_ge(y_ps[st], at(turn, 1, 1))
                    if layer == 0:
                        residual(st, turn, 1, x_mid[st], x_next[st], xout_ok[st])
                    else:
                        dve.wait_ge(y_stored[st], at(it, 16, 16))
                        residual(st, turn, 1, x_mid[st], x_fin[st], xout_ok[st])

            turns(dve, step, first)

        @block.tensor
        def _(pe):
            def first(name, k):
                if name == "ada":
                    pe.wait_ge(silu_ok, 1)
                    pe.wait_ge(wa_in[k], 16)
                    for n in range(2):
                        for c in range(2):
                            last = nc.tensor.matmul(ps[k][0:MREP, n, 0:MOD // 2], sc_sb[:, c, :],
                                                    wa_sb[k][:, c, n * MOD // 2:(n + 1) * MOD // 2],
                                                    start=(c == 0), stop=(c == 1))
                    last.then_inc(ada_ps[k], 1)

            first("ada", 0)
            pe.wait_ge(sel_ok, 1)
            pe.wait_ge(consts_ok, 2)
            pe.wait_ge(ones_ok, 9)

            def modulation(layer, st, it, at_b, cols):
                for b in range(2):
                    n = cols.stop - cols.start
                    last = nc.tensor.matmul(at_b(b), sel[:, bass.ds(first_row(st, it) + b, 1), :].rearrange("p a t -> p (a t)"),
                                            mod_b[layer][:, cols], start=True, stop=True)
                return last

            def transpose_h(st, n):
                for b in range(2):
                    dst = ps[st][0:KR, turned_bank(n, b), 0:TOK].bitcast(F16).rearrange("p (c t) -> p c t", c=CH)
                    for c in range(CH):
                        last = nc.tensor.transpose(dst[:, c, :],
                                                   h_cat[st][:, b, c * KR:(c + 1) * KR], ident16[:, :])
                    last.then_inc(hT_ps[st], 1)

            def stacked(out, layer, st, cols):
                for c in range(CH):
                    last = nc.tensor.matmul(out, w16[layer][:, c, cols], hT[st][:, c, :], start=(c == 0), stop=(c == CH - 1))
                return last

            def q_and_k(layer, st, gp):
                for n in range(2):
                    g = 2 * gp + n
                    last = stacked(ps[st][:, gp, n * TOK:(n + 1) * TOK], layer, st, slice(g * 128, (g + 1) * 128))
                last.then_inc(qk_ps[st], 1)

            def scores(layer, st, u):
                b, r = u // NJ, SLOT * (u % NJ)
                ts = slice(b * T, (b + 1) * T)
                if layer == 0:
                    nc.tensor.matmul(ps[st][:, u % 4, :], identb[:, :], causal[:, :, :], start=True, stop=False,
                                     skip_group_check=True)
                for g in range(NG):
                    last = nc.tensor.matmul(ps[st][:, u % 4, g * 128:(g + 1) * 128], qkT[st][r:r + PARTS, g, ts],
                                            qkT[st][r:r + PARTS, NG + g, ts], start=(layer == 1), stop=True,
                                            skip_group_check=True)
                last.then_inc(s_ps[st], 1)

            def scores_by_key(st, u):
                b, r = u // NJ, SLOT * (u % NJ)
                ts = slice(b * T, (b + 1) * T)
                for g in range(NG):
                    last = nc.tensor.matmul(ps[st][:, u % 2, g * 128:(g + 1) * 128],
                                            qkT[st][r:r + MROW + 1, NG + g, ts], qkT[st][r:r + MROW + 1, g, ts],
                                            start=True, stop=True, skip_group_check=True)
                last.then_inc(st_ps[st], 1)

            def values(st, u):
                b, j = u // NJ, u % NJ
                for g in range(NG):
                    last = nc.tensor.matmul(ps[st][SLOT * j:SLOT * j + HD + 1, 2, g * 128:(g + 1) * 128],
                                            v_aug[st][:, b, NJ * g + j, :], probs[st][:, u % NPROB, g, :],
                                            start=True, stop=True, skip_group_check=True)
                last.then_inc(av_ps[st], 1)

            def maxima(st, b):
                dst = ps[st][0:NJ, 3 - b, 0:256].bitcast(F16).rearrange("p (g q) -> p g q", g=NG)
                for g in range(NG):
                    last = nc.tensor.transpose(dst[:, g, :], mneg[st][:, b, g, :], ident16[:, :])
                last.then_inc(mT_ps[st], 1)

            def by_query(st, b):
                for g in range(NG):
                    last = nc.tensor.transpose(ps[st][:, 3 - b, g * 128:(g + 1) * 128], oT[st][:, g, :], ident[:, :])
                last.then_inc(on_ps[st], 1)

            def by_channel(st, b):
                for c in range(2):
                    last = nc.tensor.transpose(ps[st][0:HALF + 1, 3 - b, c * 128:(c + 1) * 128],
                                               o_nat[st][:, b, c, :], ident[:, :])
                last.then_inc(onT_ps[st], 1)

            def step(stage, k, layer, st, it, turn):
                if stage == "norm_stats" and k == 0:
                    pe.wait_ge(mod_ok[layer], 1)
                    wait(pe, xout_ok[st], at(turn, 1, 0))
                    modulation(layer, st, it, lambda b: ps[st][:, b, 0:2 * D], slice(0, 2 * D)).then_inc(mod_ps[st], 1)
                if stage == "turn_h":
                    pe.wait_ge(hcat_ok[st], at(turn, 2, k + 1))
                    pe.wait_ge(hi2_done[st], at(turn, 2, k + 1))
                    if k == 1:
                        pe.wait_ge(gate_sb[st], at(turn, 2, 1))
                    transpose_h(st, k)
                if stage == "v":
                    pe.wait_ge(kconst_in, 32)
                    pe.wait_ge(w_ok, 8 * layer + 4)
                    for b in range(2):
                        pe.wait_ge(hT_sb[st][b], at(turn, 2, 1))
                        for c in range(CH):
                            last = nc.tensor.matmul(ps[st][:, 3, b * D:(b + 1) * D], hT[st][:, c, b * T:(b + 1) * T],
                                                    w16[layer][:, c, QK:QK + D], start=(c == 0), stop=(c == CH - 1))
                    last.then_inc(v_ps[st], 1)
                if stage == "qk":
                    if k == 3:
                        pe.wait_ge(v_sb[st], at(turn, 1, 1))
                    q_and_k(layer, st, k)
                if stage == "score":
                    if k == 0:
                        pe.wait_ge(qk_ok[st], at(turn, 4, 4))
                    if k >= 4:
                        pe.wait_ge(mx_ok[st], at(turn, UNITS, k - 3))
                    if k == 7:
                        pe.wait_ge(mT_sb[st], at(turn, 2, 1))
                    scores(layer, st, k)
                if stage == "maxima":
                    pe.wait_ge(mneg_ok[st], at(turn, 2, k + 1))
                    maxima(st, k)
                if stage == "weight":
                    if k == 0:
                        pe.wait_ge(mx_ok[st], at(turn, UNITS, 6))
                    if k >= 2:
                        pe.wait_ge(exp_ok[st], at(turn, UNITS, k - 1))
                    pe.wait_ge(m_moved[st][k // NJ], at(turn, 16, 16))
                    scores_by_key(st, k)
                if stage == "value":
                    if layer == 0:
                        pe.wait_ge(cut_ok[st], at(it, UNITS, k + 1))
                    else:
                        pe.wait_ge(exp_ok[st], at(turn, UNITS, k + 1))
                    if k == 0:
                        pe.wait_ge(mT_sb[st], at(turn, 2, 2))
                    if k == NJ:
                        pe.wait_ge(o_sb[st], at(turn, 2, 1))
                    values(st, k)
                if stage == "by_query":
                    pe.wait_ge(o_sb[st], at(turn, 2, k + 1))
                    by_query(st, k)
                if stage == "by_channel":
                    pe.wait_ge(on_ok[st], at(turn, 4, 2 * k + 2))
                    by_channel(st, k)
                if stage == "gate":
                    if k == 0:
                        pe.wait_ge(exp_ok[st], at(turn, UNITS, UNITS))
                    else:
                        pe.wait_ge(f_sb[st], at(turn, 3, 1))
                    modulation(layer, st, it, lambda b: ps[st][:, 1, b * D:(b + 1) * D],
                               slice((3 * k + 2) * D, (3 * k + 3) * D)).then_inc(gate_ps[st], 1)
                if stage == "project":
                    pe.wait_ge(onT_sb[st], at(turn, 2, 2))
                    pe.wait_ge(wp_in[layer], 32)
                    for b in range(2):
                        for c in range(2):
                            rows = HALF + 1 - c
                            last = nc.tensor.matmul(ps[st][:, 0, b * D:(b + 1) * D], onT[st][0:rows, b, c, :],
                                                    wp_sb[layer][0:rows, c, :], start=(c == 0), stop=(c == 1))
                    last.then_inc(pj_ps[st], 1)
                    modulation(layer, st, it, lambda b: ps[st][:, 2 + b, 0:2 * D],
                               slice(3 * D, 5 * D)).then_inc(mod_ps[st], 1)
                if stage == "hidden":
                    if k == 0:
                        pe.wait_ge(hT_sb[st][0], at(turn, 2, 2))
                        pe.wait_ge(hT_sb[st][1], at(turn, 2, 2))
                        pe.wait_ge(w_ok, 8 * layer + 8)
                    for m in range(2 * k, min(2 * k + 2, FCH)):
                        rows = 128 if m < FCH - 1 else FLAST
                        w0 = QK + D + 128 * m
                        last = stacked(ps[st][0:rows, 1 + k, (m % 2) * TOK:(m % 2 + 1) * TOK], layer, st,
                                       slice(w0, w0 + rows))
                    last.then_inc(f_ps[st], 1)
                if stage == "mlp_out":
                    pe.wait_ge(f_sb[st], at(turn, 3, 3))
                    for b in range(2):
                        for m in range(FCH):
                            rows = 128 if m < FCH - 1 else FLAST + 1
                            last = nc.tensor.matmul(ps[st][:, 0, b * D:(b + 1) * D], ffT[st][0:rows, m, b * T:(b + 1) * T],
                                                    w2_sb[layer][0:rows, m, :], start=(m == 0), stop=(m == FCH - 1))
                    last.then_inc(y_ps[st], 1)

            turns(pe, step, first)


def _layout(inputs):
    import numpy as np

    f = {k: np.asarray(v) for k, v in inputs.items()}

    def cat(w, bias):
        rows = np.concatenate([w, w, w, bias[None], bias[None], np.zeros((CAT - 3 * D - 2, RAWCOLS), w.dtype)], axis=0)
        return np.ascontiguousarray(rows.reshape(CH, KR, RAWCOLS).transpose(1, 0, 2))

    def halves(w, bias):
        o = np.zeros((HALF + 1, 2, w.shape[1]), w.dtype)
        o[:HALF] = w.reshape(2, HALF, -1).transpose(1, 0, 2)
        o[HALF, 0] = bias
        return o

    def hidden(w, bias):
        o = np.zeros((FCH * 128, w.shape[1]), w.dtype)
        o[:FF] = w
        o[FF] = bias
        return np.ascontiguousarray(o.reshape(FCH, 128, -1).transpose(1, 0, 2))

    a = {"x": f["x"]}
    w = np.concatenate([f["L0_cond_Wq"], f["L0_cond_Wk"], f["L0_cond_Wv"], f["L0_cond_W1"]], axis=1)
    a["w_cat0"] = cat(w, np.concatenate([np.zeros(3 * D, w.dtype), f["L0_cond_b1"]]))
    a["w_cat1"] = cat(np.concatenate([f["L1_cond_W_qkv"], f["L1_cond_W_fc1"]], axis=1),
                      np.concatenate([f["L1_cond_b_qkv"], f["L1_cond_b_fc1"]]))
    a["w_proj0"] = halves(f["L0_cond_Wp"], f["L0_cond_bp"])
    a["w_proj1"] = halves(f["L1_cond_W_proj"], f["L1_cond_b_proj"])
    a["w_fc2_0"] = hidden(f["L0_cond_W2"], f["L0_cond_b2"])
    a["w_fc2_1"] = hidden(f["L1_cond_W_fc2"], f["L1_cond_b_fc2"])
    a["w_ada0"] = halves(f["L0_cond_Wa"], f["L0_cond_ba"])
    a["w_ada1"] = halves(f["L1_cond_W_ada"], f["L1_cond_b_ada"])
    c = f["cond_1152"]
    c_rep = np.zeros((HALF + 1, 2, MREP), c.dtype)
    for p in range(2):
        c_rep[:HALF, :, 32 * p:32 * p + B] = c.T.reshape(2, HALF, B).transpose(1, 0, 2)
    a["c_rep"] = c_rep
    r = np.arange(CAT).reshape(CH, KR).T
    low = ((r >= D) & (r < 2 * D)) | (r == 3 * D + 1)
    a["wmask"] = np.ascontiguousarray(np.where(low, WS, 0.0).astype(np.float32))
    slot = np.arange(128) % SLOT
    q_low = (slot >= 2 * HD) & (slot < 3 * HD)
    k_low = (slot >= HD) & (slot < 2 * HD)
    a["qkmask"] = np.stack([np.where(q_low, 1 / WS, 0.0), np.where(k_low, 1 / WS, 0.0)], axis=1).astype(np.float32)
    a["batch_sel"] = ((np.arange(MREP)[:, None] % 32 == np.arange(B)[None])
                      & (np.arange(MREP)[:, None] < 64)).astype(np.float32)
    a["k_const"] = np.full((1, H, 1), MS * WS, np.float16)
    return a


def kernel(**inputs):
    import concourse.bacc as bacc
    import numpy as np
    from concourse.bass_utils import run_bass_kernel_spmd

    nc = bacc.Bacc("TRN2", target_bir_lowering=False, num_devices=1)
    arrays = _layout(inputs)
    ap = {n: nc.dram_tensor(n + "_dram", a.shape, mybir.dt.from_np(a.dtype), kind="ExternalInput").ap()
          for n, a in arrays.items()}
    out = nc.dram_tensor("out_dram", (B, T, D), F32, kind="ExternalOutput").ap()
    two_layer_kernel(nc, ap["x"], ap["c_rep"], [ap["w_cat0"], ap["w_cat1"]], [ap["w_proj0"], ap["w_proj1"]],
                     [ap["w_fc2_0"], ap["w_fc2_1"]], [ap["w_ada0"], ap["w_ada1"]], ap["wmask"], ap["qkmask"],
                     ap["batch_sel"], ap["k_const"], out)
    r = run_bass_kernel_spmd(nc, [{n + "_dram": a for n, a in arrays.items()}], core_ids=[0])
    return np.asarray(r.results[0]["out_dram"])
```
